# Optimizing a Trainium2 kernel written in Bass

```python
import numpy as np
import jax
import jax.numpy as jnp

def _softmax(x, axis=-1):
    return jax.nn.softmax(x, axis=axis)

def _gelu(x):
    return jax.nn.gelu(x, approximate=True)

def _silu(x):
    return jax.nn.silu(x)

def _sigmoid(x):
    return jax.nn.sigmoid(x)

def _layernorm(x, axis=-1, eps=1e-05):
    m = jnp.mean(x, axis=axis, keepdims=True)
    v = jnp.var(x, axis=axis, keepdims=True)
    return (x - m) / jnp.sqrt(v + eps)

def _scatter_add(tgt, idx, src, axis=0):
    return tgt.at[idx].add(src)

def _segment_sum(src, seg, n):
    return jax.ops.segment_sum(src, seg, n)
kernel_name = 'mk_xattn_ffn_d1_seqx_r8_4775ad'

def setup_inputs(seed: int=0):
    np.random.seed(seed)
    _w = jnp.asarray

    def _rec_inputs():
        import jax
        import jax.numpy as jnp
        _rk = jax.random.key(seed)
        x = 0.0003765 + 1 * jax.random.normal(jax.random.fold_in(_rk, 1), (128, 64, 128), jnp.float32)
        _lenS = 64 - jax.random.randint(jax.random.fold_in(_rk, 7), (128,), 0, max(1, 64 // 4) + 1, jnp.int32)
        _lenS2 = 64 - jax.random.randint(jax.random.fold_in(_rk, 8), (128,), 0, max(1, 64 // 4) + 1, jnp.int32)
        _ctx_1024P = jax.random.normal(jax.random.fold_in(_rk, 11), (128, 16, 128), jnp.float32)
        _ctx_1024c = jax.random.dirichlet(jax.random.fold_in(_rk, 511), 0.3 * jnp.ones((16,), jnp.float32), (128, 64))
        _ctx_1024t = jnp.einsum('bsk,bkd->bsd', _ctx_1024c, _ctx_1024P)
        _ctx_1024t = _ctx_1024t * jax.lax.rsqrt(jnp.mean(jnp.square(_ctx_1024t)) + 1e-12) * 0.953939
        ctx_1024 = -0.000292821 + 1.00034 * (_ctx_1024t + 0.3 * jax.random.normal(jax.random.fold_in(_rk, 611), (128, 64, 128), jnp.float32))
        return (x, ctx_1024)
    x, ctx_1024 = _rec_inputs()

    def _L0_xattn_setup():
        import jax, jax.numpy as jnp
        import numpy as np
        NUM_HEADS = 16

        def _split_heads(x, num_heads):
            B, S, H = x.shape
            dh = H // num_heads
            return x.reshape(B, S, dh, num_heads).transpose(0, 3, 1, 2)
        key = jax.random.key(seed)
        ks = jax.random.split(key, 11)
        B, S, D, H = (2, 256, 128, 128)
        s = lambda k, shape, scale=1.0: jax.random.normal(k, shape, dtype=jnp.float32) * scale
        return {'KEY': s(ks[0], (B, S, D)), 'VALUE': s(ks[1], (B, S, D)), 'QUERY': s(ks[2], (B, S, D)), 'Wk_w': s(ks[3], (H, D), 0.02), 'Wk_b': s(ks[4], (H,), 0.02), 'Wq_w': s(ks[5], (H, D), 0.02), 'Wq_b': s(ks[6], (H,), 0.02), 'Wv_w': s(ks[7], (H, D), 0.02), 'Wv_b': s(ks[8], (H,), 0.02), 'Wo_w': s(ks[9], (H, H), 0.02), 'Wo_b': s(ks[10], (H,), 0.02)}
    _L0_xattn_all = _L0_xattn_setup()
    _L0_xattn_in = {k: v for k, v in _L0_xattn_all.items() if k in ('Wk_w', 'Wk_b', 'Wq_w', 'Wq_b', 'Wv_w', 'Wv_b', 'Wo_w', 'Wo_b')}
    del _L0_xattn_all

    def _L0_ffn_setup():
        import jax, jax.numpy as jnp
        import numpy as np
        GROUP = 16
        EPS = 1e-05

        def _dequant(q, scale):
            w = q.astype(jnp.float32) / 7.5 - 1.0
            return w * jnp.repeat(scale, GROUP, axis=1)

        def _qlora_linear(x, q, scale, bias, la, lb):
            w = _dequant(q, scale)
            base = jnp.einsum('btd,od->bto', x, w) + bias
            lora = jnp.einsum('btr,or->bto', jnp.einsum('btd,rd->btr', x, la), lb)
            return base + lora

        def _layernorm(x, g, b):
            mu = jnp.mean(x, axis=-1, keepdims=True)
            var = jnp.mean(jnp.square(x - mu), axis=-1, keepdims=True)
            return (x - mu) * jax.lax.rsqrt(var + EPS) * g + b
        key = jax.random.key(seed)
        ks = jax.random.split(key, 6)
        D, R, B, T = (128, 32, 8, 512)
        x = jax.random.normal(ks[0], (B, T, D), dtype=jnp.float32)
        qweights = jax.random.randint(ks[1], (6, D, D), 0, 16, dtype=jnp.int32)
        scales = jax.random.uniform(ks[2], (6, D, D // GROUP), dtype=jnp.float32)
        biases = jax.random.normal(ks[3], (6, D), dtype=jnp.float32) * 0.02
        lora_a = jax.random.normal(ks[4], (6, R, D), dtype=jnp.float32) * 0.02
        lora_b = jax.random.normal(ks[5], (6, D, R), dtype=jnp.float32) * 0.02
        ln_gamma = jnp.ones((3, D), dtype=jnp.float32)
        ln_beta = jnp.zeros((3, D), dtype=jnp.float32)
        return {'x': x, 'qweights': qweights, 'scales': scales, 'biases': biases, 'lora_a': lora_a, 'lora_b': lora_b, 'ln_gamma': ln_gamma, 'ln_beta': ln_beta}
    _L0_ffn_all = _L0_ffn_setup()
    _L0_ffn_in = {k: v for k, v in _L0_ffn_all.items() if k in ('qweights', 'scales', 'biases', 'lora_a', 'lora_b', 'ln_gamma', 'ln_beta')}
    del _L0_ffn_all
    return {'x': x, 'ctx_1024': ctx_1024, 'L0_xattn_Wk_w': _L0_xattn_in['Wk_w'], 'L0_xattn_Wk_b': _L0_xattn_in['Wk_b'], 'L0_xattn_Wq_w': _L0_xattn_in['Wq_w'], 'L0_xattn_Wq_b': _L0_xattn_in['Wq_b'], 'L0_xattn_Wv_w': _L0_xattn_in['Wv_w'], 'L0_xattn_Wv_b': _L0_xattn_in['Wv_b'], 'L0_xattn_Wo_w': _L0_xattn_in['Wo_w'], 'L0_xattn_Wo_b': _L0_xattn_in['Wo_b'], 'L0_ffn_qweights': _L0_ffn_in['qweights'], 'L0_ffn_scales': _L0_ffn_in['scales'], 'L0_ffn_biases': _L0_ffn_in['biases'], 'L0_ffn_lora_a': _L0_ffn_in['lora_a'], 'L0_ffn_lora_b': _L0_ffn_in['lora_b'], 'L0_ffn_ln_gamma': _L0_ffn_in['ln_gamma'], 'L0_ffn_ln_beta': _L0_ffn_in['ln_beta']}

def reference(x, ctx_1024, L0_xattn_Wk_w, L0_xattn_Wk_b, L0_xattn_Wq_w, L0_xattn_Wq_b, L0_xattn_Wv_w, L0_xattn_Wv_b, L0_xattn_Wo_w, L0_xattn_Wo_b, L0_ffn_qweights, L0_ffn_scales, L0_ffn_biases, L0_ffn_lora_a, L0_ffn_lora_b, L0_ffn_ln_gamma, L0_ffn_ln_beta):
    import jax
    import jax.numpy as jnp

    def _L0_xattn_ref(KEY, VALUE, QUERY, Wk_w, Wk_b, Wq_w, Wq_b, Wv_w, Wv_b, Wo_w, Wo_b):
        import jax, jax.numpy as jnp
        import numpy as np
        NUM_HEADS = 16

        def _split_heads(x, num_heads):
            B, S, H = x.shape
            dh = H // num_heads
            return x.reshape(B, S, dh, num_heads).transpose(0, 3, 1, 2)
        nh = NUM_HEADS
        k = _split_heads(KEY @ Wk_w.T + Wk_b, nh)
        q = _split_heads(QUERY @ Wq_w.T + Wq_b, nh)
        v = _split_heads(VALUE @ Wv_w.T + Wv_b, nh)
        dh = q.shape[-1]
        score = jnp.einsum('bhij,bhkj->bhik', k, q) / jnp.sqrt(jnp.asarray(dh, k.dtype))
        attn = jax.nn.softmax(score, axis=1)
        out = jnp.einsum('bhik,bhij->bhjk', attn, v)
        B = out.shape[0]
        out = out.transpose(0, 2, 1, 3).reshape(B, -1, out.shape[-1]).transpose(0, 2, 1)
        res = out @ Wo_w.T + Wo_b
        return res

    def _L0_ffn_ref(x, qweights, scales, biases, lora_a, lora_b, ln_gamma, ln_beta):
        import jax, jax.numpy as jnp
        import numpy as np
        GROUP = 16
        EPS = 1e-05

        def _dequant(q, scale):
            w = q.astype(jnp.float32) / 7.5 - 1.0
            return w * jnp.repeat(scale, GROUP, axis=1)

        def _qlora_linear(x, q, scale, bias, la, lb):
            w = _dequant(q, scale)
            base = jnp.einsum('btd,od->bto', x, w) + bias
            lora = jnp.einsum('btr,or->bto', jnp.einsum('btd,rd->btr', x, la), lb)
            return base + lora

        def _layernorm(x, g, b):
            mu = jnp.mean(x, axis=-1, keepdims=True)
            var = jnp.mean(jnp.square(x - mu), axis=-1, keepdims=True)
            return (x - mu) * jax.lax.rsqrt(var + EPS) * g + b
        h = x
        for blk in range(3):
            i0, i1 = (2 * blk, 2 * blk + 1)
            y = _qlora_linear(h, qweights[i0], scales[i0], biases[i0], lora_a[i0], lora_b[i0])
            y = _layernorm(y, ln_gamma[blk], ln_beta[blk])
            y = jax.nn.gelu(y, approximate=False)
            y = _qlora_linear(y, qweights[i1], scales[i1], biases[i1], lora_a[i1], lora_b[i1])
            h = y + h
        return h
    x = x + _L0_xattn_ref(ctx_1024, ctx_1024, _layernorm(x, axis=-1), L0_xattn_Wk_w, L0_xattn_Wk_b, L0_xattn_Wq_w, L0_xattn_Wq_b, L0_xattn_Wv_w, L0_xattn_Wv_b, L0_xattn_Wo_w, L0_xattn_Wo_b)
    x = x + _L0_ffn_ref(_layernorm(x, axis=-1), L0_ffn_qweights, L0_ffn_scales, L0_ffn_biases, L0_ffn_lora_a, L0_ffn_lora_b, L0_ffn_ln_gamma, L0_ffn_ln_beta)
    return x

_drawn_inputs = setup_inputs


def setup_inputs(seed=0):
    import zlib

    import numpy as np

    out = dict(_drawn_inputs(seed))
    spreads = {'L0_ffn_ln_gamma': (1.0, 0.2), 'L0_ffn_ln_beta': (0.0, 0.1)}
    factors = {'L0_xattn_Wk_w': 8.0,
     'L0_xattn_Wk_b': 8.0,
     'L0_xattn_Wq_w': 8.0,
     'L0_xattn_Wq_b': 8.0,
     'L0_xattn_Wv_b': 2.728,
     'L0_ffn_biases': 5.181,
     'L0_ffn_lora_a': 5.257,
     'L0_ffn_lora_b': 5.344}
    for name, (base, spread) in spreads.items():
        noise = np.random.default_rng([zlib.crc32(name.encode()), seed]).standard_normal(out[name].shape)
        drawn = base * np.exp(spread * noise) if base else spread * noise
        out[name] = jnp.asarray(drawn.astype(out[name].dtype))
    for name, factor in factors.items():
        out[name] = (out[name] * factor).astype(out[name].dtype)
    return out
```

```python
from contextlib import ExitStack

import concourse.bass as bass
from concourse import mybir

F32 = mybir.dt.float32
F16 = mybir.dt.float16
BF16 = mybir.dt.bfloat16
I32 = mybir.dt.int32
ALU = mybir.AluOpType
ACT = mybir.ActivationFunctionType
AX_X = mybir.AxisListType.X

BATCH, SEQ, D = 128, 64, 128
HEADS = 16
DH = D // HEADS
TOKENS = BATCH * SEQ
P = 128
TILE = P
CHUNK = 512
TPC = CHUNK // TILE
NCHUNK = TOKENS // CHUNK
PPC = CHUNK // (2 * SEQ)
GROUPS = 4
SLOTS = HEADS // GROUPS
TERMS = 4
GROUP = 16
NSC = D // GROUP
RANK = 32
NLIN = 6
NBLK = 3
EPS = 1e-5
SCALE = 1.0 / (DH ** 0.5)
STACK_DMAS = TERMS * SLOTS + TERMS

ROW_BQ, ROW_BK, ROW_BV, ROW_BO = 0, 1, 2, 3
ROW_BL = 4
ROW_GAMMA = ROW_BL + NLIN
ROW_BETA = ROW_GAMMA + NBLK
NROWS = ROW_BETA + NBLK
BIAS_ROWS = [ROW_BV, ROW_BO, ROW_BL, ROW_BL + 2, ROW_BL + 4]

STAGES = 5


def build(nc, x, ctx_in, wk, bk, wq, bq, wv, bv, wo, bo, qw, qs, qb, la, lb, gamma, beta, out):
    x_t = x.rearrange("b s d -> (b s) d").rearrange("(c t p) d -> c p t d", t=TPC, p=P)
    ctx_t = ctx_in.rearrange("b s d -> (b s) d").rearrange("(c t p) d -> c p t d", t=TPC, p=P)
    out_t = out.rearrange("b s d -> (b s) d").rearrange("(c t p) d -> c p t d", t=TPC, p=P)
    x_pt = x.rearrange("b s d -> (b s) d").rearrange("(c t p) d -> p c t d", t=TPC, p=P)
    parts_dram = nc.dram_tensor("qk_parts", [NCHUNK, 2, 2, P, CHUNK], F16, kind="Internal").ap()

    with ExitStack() as es:
        def sb(name, shape, dt=F32):
            return es.enter_context(nc.sbuf_tensor(name, shape, dt))

        def ps(name, shape, dt=F32):
            return es.enter_context(nc.psum_tensor(name, shape, dt))

        def sem(name):
            return es.enter_context(nc.semaphore(name))

        ident = sb("ident", [P, P])
        ident_bf = sb("ident_bf", [P, P], BF16)
        neg_ident = sb("neg_ident", [P, P], F16)
        minus_half = sb("minus_half", [P, TPC])
        w_in = {k: sb("w_in_" + k, [P, P]) for k in "qkvo"}
        rows = sb("rows", [NROWS, P])
        rows_h = sb("rows_h", [NROWS, P])
        qw_in = sb("qw_in", [P, NLIN, P], I32)
        qs_in = sb("qs_in", [P, NLIN, NSC])
        la_in = [sb("la_in0", [P, P]), sb("la_in1", [2 * RANK, P])]
        lb_in = sb("lb_in", [P, NLIN, RANK])
        w_t = {k: sb("w_t_" + k, [P, P]) for k in "qkv"}
        wo_split = sb("wo_split", [P, 2, 2, P])
        wo_t = sb("wo_t", [P, 2, 2, P])
        cols = sb("cols", [P, NROWS])
        cols_h = sb("cols_h", [P, NROWS])
        row_mid = sb("row_mid", [NROWS, P], BF16)
        row_r1 = sb("row_r1", [NROWS, P])
        row_r2 = sb("row_r2", [NROWS, P])
        bias3 = sb("bias3", [P, P], BF16)
        pick = sb("pick", [P, NROWS], BF16)
        pick_a = sb("pick_a", [P, NROWS])
        pick_row = sb("pick_row", [P, len(BIAS_ROWS), P], BF16)
        w_deq = sb("w_deq", [P, NLIN, P])
        w_eff = sb("w_eff", [P, NLIN, P])
        lb_t = [sb("lb_t0", [P, P]), sb("lb_t1", [2 * RANK, P])]
        lin_t = sb("lin_t", [P, NLIN, P])
        x_all = sb("x_all", [P, NCHUNK, TPC, D])
        ctx_sb = [sb(f"ctx_sb{i}", [P, TPC, D]) for i in range(2)]
        stats = sb("stats", [P, TPC, 6])
        agg = sb("agg", [P, 4, TPC])
        negmean = sb("negmean", [P, TPC])
        veps = sb("veps", [P, TPC])
        rstd = sb("rstd", [P, TPC])
        nmr = sb("nmr", [P, TPC])
        xln = sb("xln", [P, TPC, D])
        xln_t = sb("xln_t", [P, CHUNK])
        ctx_tr = [sb(f"ctx_tr{i}", [P, CHUNK]) for i in range(2)]
        parts = [sb(f"parts{i}", [P, 2, 2, CHUNK], F16) for i in range(2)]
        k_stack = [sb(f"k_stack{i}", [P, GROUPS, CHUNK], F16) for i in range(2)]
        q_stack = [sb(f"q_stack{i}", [P, GROUPS, SLOTS, CHUNK], F16) for i in range(2)]
        v_diag = [sb(f"v_diag{i}", [P, PPC * HEADS * 32]) for i in range(2)]
        negmax = [sb(f"negmax{i}", [P, SEQ], BF16) for i in range(2)]
        probs = [sb(f"probs{i}", [P, HEADS, SEQ]) for i in range(4)]
        zsum = [sb(f"zsum{i}", [P, SEQ]) for i in range(2)]
        rz = [sb(f"rz{i}", [P, SEQ]) for i in range(2)]
        att_t = sb("att_t", [P, 2, CHUNK // 2])
        st2 = [sb(f"st2_{i}", [P, TPC, 6]) for i in range(4)]
        ag2 = [sb(f"ag2_{i}", [P, 4, TPC]) for i in range(4)]
        ve2 = [sb(f"ve2_{i}", [P, TPC]) for i in range(4)]
        nm2 = [sb(f"nm2_{i}", [P, TPC]) for i in range(4)]
        rs2 = [sb(f"rs2_{i}", [P, TPC]) for i in range(4)]
        nmr2 = [sb(f"nmr2_{i}", [P, TPC]) for i in range(4)]
        z = [sb(f"z{i}", [P, TPC, D]) for i in range(4)]
        h = [[sb(f"h{v}_{i}", [P, CHUNK]) for i in range(2)] for v in range(4)]
        g = [sb(f"g{i}", [P, CHUNK]) for i in range(3)]

        score_ps = [ps(f"score_ps{i}", [P, HEADS * SEQ]) for i in range(2)]
        att_ps = [ps(f"att_ps{i}", [P, CHUNK]) for i in range(2)]
        work0 = ps("work0", [P, CHUNK])
        work1 = ps("work1", [P, CHUNK])
        bank = [score_ps[0][:, 0:CHUNK], score_ps[0][:, CHUNK:], score_ps[1][:, 0:CHUNK], score_ps[1][:, CHUNK:],
                att_ps[0][:, :], att_ps[1][:, :], work0[:, :], work1[:, :]]

        s_wload = sem("s_wload")
        s_fload = sem("s_fload")
        s_const = sem("s_const")
        s_cast = sem("s_cast")
        s_wperm = sem("s_wperm")
        s_split = sem("s_split")
        s_tr = sem("s_tr")
        s_wready = sem("s_wready")
        s_pick = sem("s_pick")
        s_deq = sem("s_deq")
        s_lbt_ps = sem("s_lbt_ps")
        s_lbt = sem("s_lbt")
        s_lora = sem("s_lora")
        s_weff = sem("s_weff")
        s_lint_ps = sem("s_lint_ps")
        s_lint = sem("s_lint")
        s_xin = [sem(f"s_xin{i}") for i in range(3)]
        s_ctxin = [sem(f"s_ctxin{i}") for i in range(2)]
        s_aggr = sem("s_aggr")
        s_bn = sem("s_bn")
        s_stats = sem("s_stats")
        s_rstd = sem("s_rstd")
        s_nmr = sem("s_nmr")
        s_xln = sem("s_xln")
        s_xln_ps = sem("s_xln_ps")
        s_xln_t = sem("s_xln_t")
        s_ctx_ps = sem("s_ctx_ps")
        s_ctx_t = sem("s_ctx_t")
        s_q_ps, s_k_ps = sem("s_q_ps"), sem("s_k_ps")
        s_q_hi, s_k_hi = sem("s_q_hi"), sem("s_k_hi")
        s_q_rest, s_k_rest = sem("s_q_rest"), sem("s_k_rest")
        s_q_lo, s_k_lo = sem("s_q_lo"), sem("s_k_lo")
        s_q_out, s_k_out = sem("s_q_out"), sem("s_k_out")
        s_stack = [sem(f"s_stack{i}") for i in range(2)]
        s_v_ps = sem("s_v_ps")
        s_v = sem("s_v")
        s_att_t = sem("s_att_t")
        s_wo = sem("s_wo")
        s_x2 = sem("s_x2")
        s_scores = sem("s_scores")
        s_negmax = sem("s_negmax")
        s_shifted = sem("s_shifted")
        s_exp = sem("s_exp")
        s_zsum = sem("s_zsum")
        s_rz = sem("s_rz")
        s_probs = sem("s_probs")
        s_pv = sem("s_pv")
        p_bn = [sem(f"p_bn{v}") for v in range(4)]
        p_mv = [sem(f"p_mv{v}") for v in range(4)]
        p_st = [sem(f"p_st{v}") for v in range(4)]
        p_rs = [sem(f"p_rs{v}") for v in range(4)]
        p_nmr = [sem(f"p_nmr{v}") for v in range(4)]
        p_z = [sem(f"p_z{v}") for v in range(4)]
        p_zt = [sem(f"p_zt{v}") for v in range(4)]
        p_h = [sem(f"p_h{v}") for v in range(4)]
        p_g = [sem(f"p_g{v}") for v in range(4)]
        p_y = [sem(f"p_y{v}") for v in range(4)]
        p_c = [sem(f"p_c{v}") for v in range(4)]
        p_ht = sem("p_ht")
        p_out = sem("p_out")
        s_store = sem("s_store")

        def live(c):
            return not isinstance(c, int) or 0 <= c < NCHUNK

        def some(count):
            return not isinstance(count, int) or count > 0

        def query0(pair, b):
            return 256 * (pair // 2) + SEQ * (pair % 2) + TILE * b

        def chunks(eng, body):
            for c in range(-3, 2):
                body(c, c % 2, c // 2)
            with eng.Fori(1, 6) as i:
                body(2 * i, 0, i)
                body(2 * i + 1, 1, i)
            for c in range(12, NCHUNK + 2):
                body(c, c % 2, c // 2)

        def steps(eng, body):
            for t in range(0, 6):
                body(t, t % 2)
            with eng.Fori(3, 8) as i:
                body(2 * i, 0)
                body(2 * i + 1, 1)
            for t in range(16, NCHUNK + STAGES - 1):
                body(t, t % 2)

        block = es.enter_context(nc.Block())

        @block.sync
        def _(sp):
            for k, src in (("q", wq), ("k", wk)):
                sp.dma_start(w_in[k][:, :], src).then_inc(s_wload, 16)
            for r, src in ((ROW_BQ, bq), (ROW_BK, bk), (ROW_BV, bv), (ROW_BO, bo)):
                sp.dma_start(rows[r:r + 1, :], src.rearrange("(a n) -> a n", a=1)).then_inc(s_wload, 16)
            sp.dma_start(rows[ROW_BL:ROW_BL + NLIN, :], qb).then_inc(s_wload, 16)
            sp.dma_start(rows[ROW_GAMMA:ROW_GAMMA + NBLK, :], gamma).then_inc(s_wload, 16)
            sp.dma_start(rows[ROW_BETA:ROW_BETA + NBLK, :], beta).then_inc(s_wload, 16)
            for k, src in (("v", wv), ("o", wo)):
                sp.dma_start(w_in[k][:, :], src).then_inc(s_wload, 16)

            def chunk(c, par, half):
                if isinstance(c, int) and c == -2:
                    sp.dma_start(x_all[:, 2:, :, :], x_pt[:, 2:, :, :]).then_inc(s_xin[2], 16)
                    sp.dma_start(qw_in[:, :, :], qw.rearrange("l o d -> o l d")).then_inc(s_fload, 16)
                    sp.dma_start(qs_in[:, :, :], qs.rearrange("l o s -> o l s")).then_inc(s_fload, 16)
                    la_rows = la.rearrange("l r d -> (l r) d")
                    sp.dma_start(la_in[0][:, :], la_rows[0:P, :]).then_inc(s_fload, 16)
                    sp.dma_start(la_in[1][:, :], la_rows[P:, :]).then_inc(s_fload, 16)
                    sp.dma_start(lb_in[:, :, :], lb.rearrange("l o r -> o l r")).then_inc(s_fload, 16)
                if live(c + 4):
                    if live(c + 2):
                        sp.wait_ge(s_ctx_ps, c + 3)
                    sp.dma_start(ctx_sb[par][:, :, :], ctx_t[c + 4]).then_inc(s_ctxin[par], 16)
                if live(c + 2):
                    sp.wait_ge(s_q_lo, c + 3)
                    sp.dma_start(parts_dram[c + 2, 0].rearrange("l f t -> f l t"),
                                 parts[par][:, 0, :, :]).then_inc(s_q_out, 16)
                    if live(c):
                        sp.wait_ge(s_scores, PPC * (c + 1))
                    sp.wait_ge(s_k_lo, c + 3)
                    sp.dma_start(parts_dram[c + 2, 1].rearrange("l f t -> f l t"),
                                 parts[par][:, 1, :, :]).then_inc(s_k_out, 16)
                    sp.wait_ge(s_q_out, 16 * (c + 3))
                    for t in range(TERMS):
                        src = parts_dram[c + 2, 0, t % 2].rearrange("(g s j) t -> s j g t", g=GROUPS, s=SLOTS)
                        for s in range(SLOTS):
                            r = 32 * t + DH * s
                            sp.dma_start(q_stack[par][r:r + DH, :, s, :], src[s]).then_inc(s_stack[par], 16)
                    sp.wait_ge(s_k_out, 16 * (c + 3))
                    for t in range(TERMS):
                        sp.dma_start(k_stack[par][32 * t:32 * t + 32, :, :],
                                     parts_dram[c + 2, 1, t // 2].rearrange("(g r) t -> r g t", g=GROUPS)
                                     ).then_inc(s_stack[par], 16)

            sp.dma_start(x_all[:, 0, :, :], x_t[0]).then_inc(s_xin[0], 16)
            sp.dma_start(ctx_sb[0][:, :, :], ctx_t[0]).then_inc(s_ctxin[0], 16)
            sp.dma_start(x_all[:, 1, :, :], x_t[1]).then_inc(s_xin[1], 16)
            chunks(sp, chunk)

            def step(t, par):
                k = t - 4
                if live(k):
                    sp.wait_ge(p_out, k + 1)
                    sp.dma_start(out_t[k], x_all[:, k, :, :]).then_inc(s_store, 16)

            steps(sp, step)
            sp.wait_ge(s_store, 16 * NCHUNK)

        @block.gpsimd
        def _(pool):
            nc.gpsimd.memset(ident[:, :], 0.0).then_inc(s_const, 1)
            pool.wait_ge(s_const, 1)
            nc.gpsimd.affine_select(out=ident[:, :], in_=ident[:, :], compare_op=ALU.not_equal, fill=1.0, base=0,
                                    pattern=[[-1, P]], channel_multiplier=1).then_inc(s_const, 1)
            nc.gpsimd.memset(minus_half[:, :], -0.5).then_inc(s_const, 1)
            nc.gpsimd.memset(bias3[:, :], 0.0).then_inc(s_const, 1)
            nc.gpsimd.memset(wo_split[:, :, :, :], 0.0).then_inc(s_const, 1)
            for i in range(2):
                nc.gpsimd.memset(q_stack[i][:, :, :, :].bitcast(F32), 0.0).then_inc(s_const, 1)
            for i in range(2):
                nc.gpsimd.memset(v_diag[i][:, :], 0.0).then_inc(s_const, 1)

            def chunk(c, par, half):
                for p in range(PPC):
                    n = PPC * c + p
                    mc = c - (p == 0)
                    if live(mc):
                        m = n - 1
                        pool.wait_ge(s_rz, m + 1)
                        e = probs[(p - 1) % 4]
                        nc.gpsimd.tensor_tensor(e[:, :, :], e[:, :, :],
                                                rz[(p - 1) % 2][:, :].unsqueeze(1).broadcast_to([P, HEADS, SEQ]),
                                                ALU.mult).then_inc(s_probs, 1)
                    if p == 1 and live(c + 3):
                        pool.wait_ge(s_stats, c + 4)
                        if some(c + 3):
                            pool.wait_ge(s_nmr, c + 3)
                            pool.wait_ge(s_xln, c + 3)
                        nc.gpsimd.tensor_tensor(rstd[:, :], veps[:, :], minus_half[:, :], ALU.pow).then_inc(s_rstd, 1)

            chunks(pool, chunk)

            def norm_scale(v, k):
                pool.wait_ge(p_st[v], k + 1)
                if some(k):
                    pool.wait_ge(p_z[v], k)
                nc.gpsimd.tensor_tensor(rs2[v][:, :], ve2[v][:, :], minus_half[:, :], ALU.pow).then_inc(p_rs[v], 1)
                pool.wait_ge(p_rs[v], k + 1)
                nc.gpsimd.tensor_tensor(nmr2[v][:, :], nm2[v][:, :], rs2[v][:, :], ALU.mult).then_inc(p_nmr[v], 1)

            def step(t, par):
                for v, k in ((0, t), (1, t - 1), (3, t - 3), (2, t - 2)):
                    if live(k):
                        norm_scale(v, k)

            steps(pool, step)

        @block.vector
        def _(dve):
            dve.wait_ge(s_const, 2)
            nc.vector.tensor_copy(ident_bf[:, :], ident[:, :]).then_inc(s_cast, 1)
            nc.vector.tensor_scalar(neg_ident[:, :], ident[:, :], -1.0, None, ALU.mult).then_inc(s_cast, 1)
            nc.vector.tensor_tensor(pick_a[:, :], ident[:, 0:NROWS], ident[:, 32:32 + NROWS], ALU.add).then_inc(s_pick, 1)
            dve.wait_ge(s_pick, 1)
            nc.vector.tensor_tensor(pick[:, :], pick_a[:, :], ident[:, 64:64 + NROWS], ALU.add).then_inc(s_pick, 1)
            dve.wait_ge(s_pick, 2)
            for i, r in enumerate(BIAS_ROWS):
                nc.vector.tensor_copy(pick_row[:, i, :], pick[:, r:r + 1].broadcast_to([P, P])).then_inc(s_pick, 1)
            dve.wait_ge(s_wload, 16 * 11)
            dve.wait_ge(s_const, 5)
            wo_cols = w_in["o"][:, :].rearrange("p (j o u) -> p o u j", o=2, u=8)
            for o in range(2):
                for b in range(2):
                    dst = wo_split[:, o, b, :].rearrange("p (u b j) -> p b u j", u=8, b=2)
                    nc.vector.tensor_copy(dst[:, b], wo_cols[:, o]).then_inc(s_wperm, 1)
            nc.vector.tensor_copy(rows_h[:, :].rearrange("p (h j) -> p h j", j=DH),
                                  rows[:, :].rearrange("p (j h) -> p h j", j=DH)).then_inc(s_wperm, 1)
            nc.vector.tensor_copy(bias3[0:NROWS, :], rows[:, :]).then_inc(s_split, 1)
            dve.wait_ge(s_split, 1)
            nc.vector.tensor_tensor(row_r1[:, :], rows[:, :], bias3[0:NROWS, :], ALU.subtract).then_inc(s_split, 1)
            dve.wait_ge(s_split, 2)
            nc.vector.tensor_copy(bias3[32:32 + NROWS, :], row_r1[:, :]).then_inc(s_split, 1)
            nc.vector.tensor_copy(row_mid[:, :], row_r1[:, :]).then_inc(s_split, 1)
            dve.wait_ge(s_split, 4)
            nc.vector.tensor_tensor(row_r2[:, :], row_r1[:, :], row_mid[:, :],
                                    ALU.subtract).then_inc(s_split, 1)
            dve.wait_ge(s_split, 5)
            nc.vector.tensor_copy(bias3[64:64 + NROWS, :], row_r2[:, :]).then_inc(s_split, 1)

            def feed_forward_weights():
                dve.wait_ge(s_fload, 16 * 5)
                nc.vector.tensor_scalar(w_deq[:, :, :], qw_in[:, :, :], 1.0 / 7.5, -1.0, ALU.mult,
                                        ALU.add).then_inc(s_deq, 1)
                dve.wait_ge(s_deq, 1)
                nc.vector.tensor_tensor(
                    w_deq[:, :, :].rearrange("p l (s e) -> p (l s) e", e=GROUP),
                    w_deq[:, :, :].rearrange("p l (s e) -> p (l s) e", e=GROUP),
                    qs_in[:, :, :].rearrange("p l s -> p (l s)").unsqueeze(2).broadcast_to([P, NLIN * NSC, GROUP]),
                    ALU.mult).then_inc(s_deq, 1)
                dve.wait_ge(s_lbt_ps, 2)
                nc.vector.tensor_copy(lb_t[0][:, :], bank[4][:, 0:P]).then_inc(s_lbt, 1)
                nc.vector.tensor_copy(lb_t[1][:, :], bank[5][0:2 * RANK, 0:P]).then_inc(s_lbt, 1)
                dve.wait_ge(s_deq, 2)
                for i in range(NLIN):
                    dve.wait_ge(s_lora, i + 1)
                    nc.vector.tensor_tensor(w_eff[:, i, :], bank[i % 4][:, 0:P] if i < 4 else bank[i][:, 0:P],
                                            w_deq[:, i, :], ALU.add).then_inc(s_weff, 1)

            def combine(k, bn_done, step_done, used, done, st, ag, ve, nm):
                dve.wait_ge(bn_done, TPC * (k + 1))
                nc.vector.tensor_tensor(ag[:, 0, :], st[:, :, 1], st[:, :, 4], ALU.add)
                nc.vector.scalar_tensor_tensor(ag[:, 1, :], st[:, :, 2], EPS * D, st[:, :, 5], ALU.add, ALU.add)
                nc.vector.tensor_tensor(ag[:, 2, :], st[:, :, 1], st[:, :, 4], ALU.subtract).then_inc(step_done, 1)
                dve.wait_ge(step_done, 2 * k + 1)
                nc.vector.scalar_tensor_tensor(ag[:, 3, :], ag[:, 2, :], 0.25, ag[:, 2, :], ALU.mult,
                                               ALU.mult).then_inc(step_done, 1)
                dve.wait_ge(step_done, 2 * k + 2)
                if some(k):
                    dve.wait_ge(used, k)
                nc.vector.tensor_scalar(nm[:, :], ag[:, 0, :], -0.5, None, ALU.mult)
                nc.vector.scalar_tensor_tensor(ve[:, :], ag[:, 1, :], 1.0 / D, ag[:, 3, :], ALU.mult,
                                               ALU.add).then_inc(done, 1)

            def chunk(c, par, half):
                if isinstance(c, int) and c == -1:
                    feed_forward_weights()
                for p in range(PPC):
                    n = PPC * c + p
                    if live(c):
                        dve.wait_ge(s_scores, n + 1)
                        if some(n - 1):
                            dve.wait_ge(s_shifted, n - 1)
                        nc.vector.tensor_reduce(negmax[p % 2][:, :],
                                                score_ps[p % 2][:, :].rearrange("p (h k) -> p k h", k=SEQ),
                                                AX_X, ALU.max, negate=True).then_inc(s_negmax, 1)
                    if p == 0 and live(c - 2):
                        dve.wait_ge(s_wo, c - 1)
                        nc.vector.tensor_tensor(x_all[:, c - 2, :, :],
                                                work1[:, :].rearrange("p (t d) -> p t d", t=TPC),
                                                x_all[:, c - 2, :, :], ALU.add).then_inc(s_x2, 1)
                    if p == 1 and live(c + 3):
                        if isinstance(c, int) and c + 3 < 3:
                            dve.wait_ge(s_xin[c + 3], 16)
                        for t in range(TPC):
                            nc.vector.bn_stats(stats[:, t, :], x_all[:, c + 3, t, :]).then_inc(s_bn, 1)
                        combine(c + 3, s_bn, s_aggr, s_nmr, s_stats, stats, agg, veps, negmean)
                    mc = c - (p == 0)
                    if live(mc):
                        m = n - 1
                        q = (p - 1) % 2
                        dve.wait_ge(s_exp, m + 1)
                        nc.vector.tensor_reduce(zsum[q][:, :], probs[(p - 1) % 4][:, :, :].rearrange("p h k -> p k h"),
                                                AX_X, ALU.add).then_inc(s_zsum, 1)
                        dve.wait_ge(s_zsum, m + 1)
                        if some(m - 1):
                            dve.wait_ge(s_probs, m - 1)
                        nc.vector.reciprocal(rz[q][:, :], zsum[q][:, :]).then_inc(s_rz, 1)
                    if p == 2 and live(c + 3):
                        dve.wait_ge(s_rstd, c + 4)
                        if some(c + 3):
                            dve.wait_ge(s_xln, c + 3)
                        nc.vector.tensor_tensor(nmr[:, :], negmean[:, :], rstd[:, :], ALU.mult).then_inc(s_nmr, 1)

            chunks(dve, chunk)

            def norm_stats(v, k, tile):
                for t in range(TPC):
                    nc.vector.bn_stats(st2[v][:, t, :], tile(t)).then_inc(p_bn[v], 1)
                combine(k, p_bn[v], p_mv[v], p_nmr[v], p_st[v], st2[v], ag2[v], ve2[v], nm2[v])

            def step(t, par):
                if live(t):
                    if isinstance(t, int) and t == 0:
                        dve.wait_ge(s_x2, NCHUNK)
                    norm_stats(0, t, lambda i: x_all[:, t, i, :])
                for v, k in ((3, t - 4), (2, t - 3), (1, t - 2)):
                    if live(k):
                        q = (par - v - 1) % 2
                        dve.wait_ge(p_c[v], k + 1)
                        if some(k - 1):
                            if v < 3:
                                dve.wait_ge(p_h[v + 1], k - 1)
                            else:
                                dve.wait_ge(p_ht, k - 1)
                        nc.vector.scalar_tensor_tensor(h[v][q][:, :], bank[7 - v][:, :],
                                                       cols[:, ROW_BL + 2 * v - 1:ROW_BL + 2 * v],
                                                       h[v - 1][q][:, :], ALU.add, ALU.add).then_inc(p_h[v], 1)
                if live(t - 1):
                    k = t - 1
                    dve.wait_ge(p_y[1], k + 1)
                    norm_stats(1, k, lambda i: bank[7][:, TILE * i:TILE * (i + 1)])
                if live(t - 4):
                    k = t - 4
                    dve.wait_ge(p_ht, k + 1)
                    nc.vector.tensor_tensor(x_all[:, k, :, :], bank[0].rearrange("p (t d) -> p t d", t=TPC),
                                            x_all[:, k, :, :], ALU.add).then_inc(p_out, 1)
                if live(t - 3):
                    k = t - 3
                    dve.wait_ge(p_y[3], k + 1)
                    norm_stats(3, k, lambda i: bank[1][:, TILE * i:TILE * (i + 1)])
                if live(t - 2):
                    k = t - 2
                    dve.wait_ge(p_y[2], k + 1)
                    norm_stats(2, k, lambda i: bank[2][:, TILE * i:TILE * (i + 1)])

            steps(dve, step)

        @block.scalar
        def _(act):
            for i, k in enumerate("qkv"):
                act.wait_ge(s_tr, i + 1)
                nc.scalar.activation(w_t[k][:, :].rearrange("p (h j) -> p h j", j=DH),
                                     bank[i][:, 0:P].rearrange("p (j h) -> p h j", j=DH), ACT.Copy).then_inc(s_wready, 1)
            act.wait_ge(s_tr, 4)
            nc.scalar.activation(cols[:, :], bank[3][:, 0:NROWS], ACT.Copy).then_inc(s_wready, 1)
            nc.scalar.activation(cols_h[:, :], bank[3][:, NROWS:2 * NROWS], ACT.Copy).then_inc(s_wready, 1)
            act.wait_ge(s_tr, 5)
            nc.scalar.activation(wo_t[:, :, :, :].rearrange("p o b n -> p (o b n)"), bank[4], ACT.Copy).then_inc(s_wready, 1)

            act.wait_ge(s_wready, 6)

            def feed_forward_weights():
                for i in range(NLIN):
                    act.wait_ge(s_lint_ps, i + 1)
                    nc.scalar.activation(lin_t[:, i, :], bank[i][:, 0:P] if i < 4 else bank[i % 4][:, P:2 * P],
                                         ACT.Copy).then_inc(s_lint, 1)

            def chunk(c, par, half):
                if isinstance(c, int) and c == -1:
                    feed_forward_weights()

                def exponentials(p):
                    n = PPC * c + p
                    act.wait_ge(s_shifted, n + 1)
                    if some(n - 3):
                        act.wait_ge(s_pv, n - 3)
                    nc.scalar.activation(probs[p][:, :, :].rearrange("p h k -> p (h k)"), score_ps[p % 2][:, :],
                                         ACT.Exp, scale=SCALE).then_inc(s_exp, 1)

                if live(c + 2):
                    act.wait_ge(s_xln_ps, c + 3)
                    if some(c + 2):
                        act.wait_ge(s_q_ps, c + 2)
                    nc.scalar.activation(xln_t[:, :], work0[:, :], ACT.Copy).then_inc(s_xln_t, 1)
                if live(c):
                    exponentials(0)
                if live(c + 2):
                    act.wait_ge(s_ctx_ps, c + 3)
                    if some(c + 1):
                        act.wait_ge(s_v_ps, c + 1)
                    nc.scalar.activation(ctx_tr[par][:, :], work1[:, :], ACT.Copy).then_inc(s_ctx_t, 1)
                if live(c + 2):
                    act.wait_ge(s_q_ps, c + 3)
                    if some(c + 1):
                        act.wait_ge(s_q_out, 16 * (c + 1))
                    nc.scalar.activation(parts[par][:, 0, 0, :], work0[:, :], ACT.Identity,
                                         bias=cols_h[:, ROW_BQ:ROW_BQ + 1]).then_inc(s_q_hi, 1)
                if live(c):
                    exponentials(1)
                if live(c + 2):
                    act.wait_ge(s_q_rest, c + 3)
                    nc.scalar.activation(parts[par][:, 0, 1, :], work0[:, :], ACT.Identity,
                                         bias=cols_h[:, ROW_BQ:ROW_BQ + 1]).then_inc(s_q_lo, 1)
                if live(c + 2):
                    act.wait_ge(s_k_ps, c + 3)
                    if some(c + 1):
                        act.wait_ge(s_k_out, 16 * (c + 1))
                    nc.scalar.activation(parts[par][:, 1, 0, :], work1[:, :], ACT.Identity,
                                         bias=cols_h[:, ROW_BK:ROW_BK + 1]).then_inc(s_k_hi, 1)
                if live(c):
                    exponentials(2)
                if live(c - 1):
                    act.wait_ge(s_pv, PPC * c)
                    if some(c - 1):
                        act.wait_ge(s_wo, c - 1)
                    nc.scalar.activation(att_t[:, :, :].rearrange("p o t -> p (o t)"), att_ps[1 - par][:, :],
                                         ACT.Copy).then_inc(s_att_t, 1)
                if live(c + 2):
                    act.wait_ge(s_k_rest, c + 3)
                    nc.scalar.activation(parts[par][:, 1, 1, :], work1[:, :], ACT.Identity,
                                         bias=cols_h[:, ROW_BK:ROW_BK + 1]).then_inc(s_k_lo, 1)
                if live(c + 1):
                    act.wait_ge(s_v_ps, c + 2)
                    if live(c - 1):
                        act.wait_ge(s_pv, PPC * c)
                    elif isinstance(c, int) and c == -1:
                        act.wait_ge(s_const, 9)
                    for b in range(2):
                        dst = v_diag[1 - par][SEQ * b:SEQ * (b + 1), :].rearrange("p (u a e) -> p u a e", a=4, e=16)
                        ins = nc.scalar.activation(
                            dst[:, :, 0:4:3, DH * b:DH * (b + 1)],
                            work0[SEQ * b:SEQ * (b + 1), :].rearrange("p (u s j) -> p u s j", s=2, j=DH), ACT.Copy)
                    ins.then_inc(s_v, 1)
                if live(c):
                    exponentials(3)
                if live(c + 3):
                    act.wait_ge(s_nmr, c + 4)
                    act.wait_ge(s_rstd, c + 4)
                    if some(c + 3):
                        act.wait_ge(s_xln_ps, c + 3)
                    for t in range(TPC):
                        ins = nc.scalar.activation(xln[:, t, :], x_all[:, c + 3, t, :], ACT.Identity,
                                                   bias=nmr[:, t:t + 1], scale=rstd[:, t:t + 1])
                    ins.then_inc(s_xln, 1)

            chunks(act, chunk)

            def normalise(v, k, tile):
                act.wait_ge(p_nmr[v], k + 1)
                if some(k):
                    act.wait_ge(p_zt[v], k)
                for t in range(TPC):
                    ins = nc.scalar.activation(z[v][:, t, :], tile(t), ACT.Identity,
                                               bias=nmr2[v][:, t:t + 1], scale=rs2[v][:, t:t + 1])
                ins.then_inc(p_z[v], 1)

            def step(t, par):
                for v, k in ((3, t - 4), (2, t - 3), (1, t - 2)):
                    if live(k):
                        act.wait_ge(p_zt[v], k + 1)
                        if some(k):
                            act.wait_ge(p_c[v], k)
                        nc.scalar.activation(g[v - 1][:, :], bank[3 - v], ACT.Gelu,
                                             bias=cols[:, ROW_BETA + v - 1:ROW_BETA + v],
                                             scale=cols[:, ROW_GAMMA + v - 1:ROW_GAMMA + v]).then_inc(p_g[v], 1)
                if live(t - 1):
                    k = t - 1
                    act.wait_ge(p_zt[0], k + 1)
                    if some(k - 1):
                        act.wait_ge(p_h[1], k - 1)
                    nc.scalar.activation(h[0][(par - 1) % 2][:, :], bank[3], ACT.Copy).then_inc(p_h[0], 1)
                if live(t):
                    normalise(0, t, lambda i: x_all[:, t, i, :])
                if live(t - 1):
                    normalise(1, t - 1, lambda i: bank[7][:, TILE * i:TILE * (i + 1)])
                if live(t - 3):
                    normalise(3, t - 3, lambda i: bank[1][:, TILE * i:TILE * (i + 1)])
                if live(t - 2):
                    normalise(2, t - 2, lambda i: bank[2][:, TILE * i:TILE * (i + 1)])

            steps(act, step)

        @block.tensor
        def _(pe):
            pe.wait_ge(s_const, 2)
            pe.wait_ge(s_wload, 16 * 11)
            for i, k in enumerate("qkv"):
                nc.tensor.transpose(bank[i][:, 0:P], w_in[k][:, :], ident[:, :]).then_inc(s_tr, 1)
            pe.wait_ge(s_wperm, 5)
            nc.tensor.transpose(bank[3][:, 0:NROWS], rows[:, :], ident[0:NROWS, 0:NROWS])
            nc.tensor.transpose(bank[3][:, NROWS:2 * NROWS], rows_h[:, :],
                                ident[0:NROWS, 0:NROWS]).then_inc(s_tr, 1)
            for o in range(2):
                for b in range(2):
                    ins = nc.tensor.transpose(bank[4][:, P * (2 * o + b):P * (2 * o + b + 1)], wo_split[:, o, b, :],
                                              ident[:, :])
            ins.then_inc(s_tr, 1)
            pe.wait_ge(s_wready, 6)
            pe.wait_ge(s_cast, 2)
            pe.wait_ge(s_pick, 2 + len(BIAS_ROWS))
            pe.wait_ge(s_split, 6)

            def feed_forward_weights():
                pe.wait_ge(s_fload, 16 * 5)
                lb_cols = lb_in[:, :, :].rearrange("p l r -> p (l r)")
                nc.tensor.transpose(bank[4][:, 0:P], lb_cols[:, 0:P], ident[:, :]).then_inc(s_lbt_ps, 1)
                nc.tensor.transpose(bank[5][0:2 * RANK, 0:P], lb_cols[:, P:], ident[:, :]).then_inc(s_lbt_ps, 1)
                pe.wait_ge(s_lbt, 2)
                for i in range(NLIN):
                    r = RANK * (i % 4)
                    nc.tensor.matmul(bank[i][:, 0:P], lb_t[i // 4][r:r + RANK, :], la_in[i // 4][r:r + RANK, :],
                                     start=True, stop=True).then_inc(s_lora, 1)
                for i in range(NLIN):
                    pe.wait_ge(s_weff, i + 1 if i < 4 else NLIN)
                    if i >= 4:
                        pe.wait_ge(s_lint, i - 3)
                    nc.tensor.transpose(bank[i][:, 0:P] if i < 4 else bank[i % 4][:, P:2 * P], w_eff[:, i, :],
                                        ident[:, :]).then_inc(s_lint_ps, 1)

            def bias_rows(dst, which, head_major=False):
                src = bias3[:, :].rearrange("p (j h) -> p h j", j=DH) if head_major else bias3[:, :]
                src = src.unsqueeze(1).broadcast_to([P, TPC] + list(src.shape[1:]))
                nc.tensor.matmul(dst, pick_row[:, which, :], src, start=True, stop=False, skip_group_check=True)

            def chunk(c, par, half):
                if isinstance(c, int) and c == -1:
                    feed_forward_weights()
                for p in range(PPC):
                    n = PPC * c + p
                    mc, mp = (c, p + 1) if p < 3 else (c + 1, 0)
                    if live(mc):
                        m = n + 1
                        mpar = mp % 2
                        mb = par if p < 3 else 1 - par
                        if mp == 0:
                            mh = half if par == 0 else half + 1
                            pe.wait_ge(s_stack[mb], 16 * STACK_DMAS * (mh + 1))
                            if isinstance(c, int) and c == -1:
                                pe.wait_ge(s_lint, NLIN)
                        if some(m - 1):
                            pe.wait_ge(s_exp, m - 1)
                        for grp in range(GROUPS):
                            for b in range(2):
                                q0, k0 = query0(mp, b), TILE * mp + SEQ * b
                                ins = nc.tensor.matmul(
                                    score_ps[mpar][SEQ * b:SEQ * (b + 1), 256 * grp:256 * (grp + 1)],
                                    k_stack[mb][:, grp, k0:k0 + SEQ], q_stack[mb][:, grp, :, q0:q0 + SEQ],
                                    start=grp % 2 == 0, stop=False, skip_group_check=True)
                        ins.then_inc(s_scores, 1)
                    if p == 0 and live(c + 2):
                        pe.wait_ge(s_xln, c + 3)
                        if some(c + 1):
                            pe.wait_ge(s_v, c + 1)
                        for t in range(TPC):
                            ins = nc.tensor.transpose(work0[:, TILE * t:TILE * (t + 1)], xln[:, t, :], ident[:, :])
                        ins.then_inc(s_xln_ps, 1)
                    if p == 1 and live(c + 2):
                        pe.wait_ge(s_xln_t, c + 3)
                        nc.tensor.matmul(work0[:, :], w_t["q"][:, :], xln_t[:, :], start=True, stop=False,
                                         skip_group_check=True).then_inc(s_q_ps, 1)
                    if p == 2 and live(c + 2):
                        pe.wait_ge(s_ctx_t, c + 3)
                        nc.tensor.matmul(work1[:, :], w_t["k"][:, :], ctx_tr[par][:, :], start=True, stop=False,
                                         skip_group_check=True).then_inc(s_k_ps, 1)
                    if p == 3 and live(c + 1):
                        if live(c + 2):
                            pe.wait_ge(s_q_lo, c + 3)
                        elif some(c + 1):
                            pe.wait_ge(s_v, c + 1)
                        bias_rows(work0[:, :], 0, head_major=True)
                        for q in range(PPC):
                            ins = nc.tensor.matmul(work0[:, TILE * q:TILE * (q + 1)],
                                                   ctx_tr[1 - par][:, TILE * q:TILE * (q + 1)], w_t["v"][:, :],
                                                   start=False, stop=True, skip_group_check=True)
                        ins.then_inc(s_v_ps, 1)
                    if live(c):
                        pe.wait_ge(s_negmax, n + 1)
                        for o in range(2):
                            ins = nc.tensor.matmul(score_ps[p % 2][:, CHUNK * o:CHUNK * (o + 1)], ident_bf[:, :],
                                                   negmax[p % 2][:, :].unsqueeze(1).broadcast_to([P, 8, SEQ]),
                                                   start=False, stop=True, skip_group_check=True)
                        ins.then_inc(s_shifted, 1)
                    mc, mp = (c, p - 2) if p >= 2 else (c - 1, p + 2)
                    if live(mc):
                        m = n - 2
                        mb = par if p >= 2 else 1 - par
                        pe.wait_ge(s_probs, m + 1)
                        if mp == 0:
                            pe.wait_ge(s_v, mc + 1)
                            if some(mc - 1):
                                pe.wait_ge(s_att_t, mc - 1)
                        for o in range(2):
                            for s in range(2):
                                for grp in range(4):
                                    hd = 8 * o + 2 * grp + s
                                    v0 = 32 * (HEADS * mp + hd)
                                    c0 = 256 * o + SEQ * mp
                                    ins = nc.tensor.matmul(
                                        att_ps[mb][32 * grp:32 * (grp + 1), c0:c0 + SEQ], v_diag[mb][:, v0:v0 + 32],
                                        probs[mp][:, hd, :], start=(mp == 0 and o == 0 and s == 0),
                                        stop=False, skip_group_check=True, tile_position=(0, 32 * grp))
                        ins.then_inc(s_pv, 1)
                    if p == 0 and live(c + 2):
                        pe.wait_ge(s_ctxin[par], 16 * (half + 2))
                        if live(c - 2):
                            pe.wait_ge(s_x2, c - 1)
                        elif some(c + 2):
                            pe.wait_ge(s_k_lo, c + 2)
                        dst = work1[:, :].rearrange("p (u v b k) -> p u b v k", u=2, v=2, b=2)
                        for t in range(TPC):
                            ins = nc.tensor.transpose(dst[:, t // 2, t % 2], ctx_sb[par][:, t, :], ident[:, :])
                        ins.then_inc(s_ctx_ps, 1)
                    if p == 1 and live(c + 2):
                        pe.wait_ge(s_q_hi, c + 3)
                        nc.tensor.matmul(work0[:, :], neg_ident[:, :], parts[par][:, 0, 0, :], start=False, stop=True,
                                         skip_group_check=True).then_inc(s_q_rest, 1)
                    if p == 2 and live(c + 2):
                        pe.wait_ge(s_k_hi, c + 3)
                        nc.tensor.matmul(work1[:, :], neg_ident[:, :], parts[par][:, 1, 0, :], start=False, stop=True,
                                         skip_group_check=True).then_inc(s_k_rest, 1)
                    if p == 3 and live(c - 1):
                        pe.wait_ge(s_att_t, c)
                        if live(c + 2):
                            pe.wait_ge(s_k_lo, c + 3)
                        elif live(c - 2):
                            pe.wait_ge(s_x2, c - 1)
                        bias_rows(work1[:, :], 1)
                        for t in range(TPC):
                            b, u = t % 2, t // 2
                            for o in range(2):
                                ins = nc.tensor.matmul(work1[:, TILE * t:TILE * (t + 1)],
                                                       att_t[:, o, TILE * u:TILE * (u + 1)], wo_t[:, o, b, :],
                                                       start=False, stop=o == 1, skip_group_check=True)
                        ins.then_inc(s_wo, 1)

            chunks(pe, chunk)
            pe.wait_ge(s_x2, NCHUNK)

            def transpose_z(v, k, dst):
                pe.wait_ge(p_z[v], k + 1)
                for t in range(TPC):
                    ins = nc.tensor.transpose(dst[:, TILE * t:TILE * (t + 1)], z[v][:, t, :], ident[:, :])
                ins.then_inc(p_zt[v], 1)

            def first_layer(v, hk, dst):
                bias_rows(dst, 1 + v)
                for t in range(TPC):
                    ins = nc.tensor.matmul(dst[:, TILE * t:TILE * (t + 1)], hk[:, TILE * t:TILE * (t + 1)],
                                           lin_t[:, 2 * v - 2, :], start=False, stop=True, skip_group_check=True)
                ins.then_inc(p_y[v], 1)

            def step(t, par):
                if live(t - 4):
                    k = t - 4
                    if some(k):
                        pe.wait_ge(p_out, k)
                    transpose_z(3, k, bank[0])
                if live(t - 3):
                    k = t - 3
                    if some(k):
                        pe.wait_ge(p_z[3], k)
                    transpose_z(2, k, bank[1])
                if live(t - 2):
                    k = t - 2
                    if some(k):
                        pe.wait_ge(p_z[2], k)
                    transpose_z(1, k, bank[2])
                if live(t - 1):
                    k = t - 1
                    if some(k):
                        pe.wait_ge(p_h[0], k)
                    transpose_z(0, k, bank[3])
                for v, k in ((3, t - 4), (2, t - 3), (1, t - 2)):
                    if live(k):
                        pe.wait_ge(p_g[v], k + 1)
                        if some(k):
                            pe.wait_ge(p_h[v], k)
                        nc.tensor.matmul(bank[7 - v], lin_t[:, 2 * v - 1, :], g[v - 1][:, :], start=True,
                                         stop=True).then_inc(p_c[v], 1)
                if live(t - 1):
                    k = t - 1
                    pe.wait_ge(p_h[0], k + 1)
                    if some(k):
                        pe.wait_ge(p_z[1], k)
                    first_layer(1, h[0][(par - 1) % 2], bank[7])
                if live(t - 4):
                    k = t - 4
                    pe.wait_ge(p_h[3], k + 1)
                    for i in range(TPC):
                        ins = nc.tensor.transpose(bank[0][:, TILE * i:TILE * (i + 1)],
                                                  h[3][par][:, TILE * i:TILE * (i + 1)], ident[:, :])
                    ins.then_inc(p_ht, 1)
                if live(t - 3):
                    pe.wait_ge(p_h[2], t - 2)
                    first_layer(3, h[2][(par - 3) % 2], bank[1])
                if live(t - 2):
                    pe.wait_ge(p_h[1], t - 1)
                    first_layer(2, h[1][par], bank[2])

            steps(pe, step)


_INS = ["x", "ctx_1024", "L0_xattn_Wk_w", "L0_xattn_Wk_b", "L0_xattn_Wq_w", "L0_xattn_Wq_b", "L0_xattn_Wv_w",
        "L0_xattn_Wv_b", "L0_xattn_Wo_w", "L0_xattn_Wo_b", "L0_ffn_qweights", "L0_ffn_scales", "L0_ffn_biases",
        "L0_ffn_lora_a", "L0_ffn_lora_b", "L0_ffn_ln_gamma", "L0_ffn_ln_beta"]


def kernel(**inputs):
    import numpy as _np
    import concourse.bacc as _bacc
    from concourse import mybir as _mybir
    from concourse.bass_utils import run_bass_kernel_spmd as _run

    nc = _bacc.Bacc("TRN2", target_bir_lowering=False, num_devices=1)
    arrays, args = {}, []
    for name in _INS:
        a = _np.ascontiguousarray(inputs[name])
        arrays[f"in_{name}"] = a
        args.append(nc.dram_tensor(f"in_{name}", a.shape, _mybir.dt.from_np(a.dtype), kind="ExternalInput").ap())
    args.append(nc.dram_tensor("out_0", (BATCH, SEQ, D), F32, kind="ExternalOutput").ap())
    build(nc, *args)
    r = _run(nc, [arrays], core_ids=[0])
    return r.results[0]["out_0"]
```

```python
from contextlib import ExitStack

import concourse.bass as bass
from concourse import mybir

F32 = mybir.dt.float32
F16 = mybir.dt.float16
BF16 = mybir.dt.bfloat16
I32 = mybir.dt.int32
ALU = mybir.AluOpType
ACT = mybir.ActivationFunctionType
AX_X = mybir.AxisListType.X

BATCH, SEQ, D = 128, 64, 128
HEADS = 16
DH = D // HEADS
TOKENS = BATCH * SEQ
P = 128
TILE = P
CHUNK = 512
TPC = CHUNK // TILE
NCHUNK = TOKENS // CHUNK
PPC = CHUNK // (2 * SEQ)
GROUPS = 4
SLOTS = HEADS // GROUPS
TERMS = 4
GROUP = 16
NSC = D // GROUP
RANK = 32
NLIN = 6
NBLK = 3
EPS = 1e-5
SCALE = 1.0 / (DH ** 0.5)
STACK_DMAS = TERMS * SLOTS + TERMS

ROW_BQ, ROW_BK, ROW_BV, ROW_BO = 0, 1, 2, 3
ROW_BL = 4
ROW_GAMMA = ROW_BL + NLIN
ROW_BETA = ROW_GAMMA + NBLK
NROWS = ROW_BETA + NBLK
BIAS_ROWS = [ROW_BV, ROW_BO, ROW_BL, ROW_BL + 2, ROW_BL + 4]

STAGES = 8


def build(nc, x, ctx_in, wk, bk, wq, bq, wv, bv, wo, bo, qw, qs, qb, la, lb, gamma, beta, out):
    x_t = x.rearrange("b s d -> (b s) d").rearrange("(c t p) d -> c p t d", t=TPC, p=P)
    ctx_t = ctx_in.rearrange("b s d -> (b s) d").rearrange("(c t p) d -> c p t d", t=TPC, p=P)
    out_t = out.rearrange("b s d -> (b s) d").rearrange("(c t p) d -> c p t d", t=TPC, p=P)
    x_pt = x.rearrange("b s d -> (b s) d").rearrange("(c t p) d -> p c t d", t=TPC, p=P)
    parts_dram = nc.dram_tensor("qk_parts", [NCHUNK, 2, 2, P, CHUNK], F16, kind="Internal").ap()

    with ExitStack() as es:
        def sb(name, shape, dt=F32):
            return es.enter_context(nc.sbuf_tensor(name, shape, dt))

        def ps(name, shape, dt=F32):
            return es.enter_context(nc.psum_tensor(name, shape, dt))

        def sem(name):
            return es.enter_context(nc.semaphore(name))

        ident = sb("ident", [P, P])
        ident_bf = sb("ident_bf", [P, P], BF16)
        neg_ident = sb("neg_ident", [P, P], F16)
        minus_half = sb("minus_half", [P, 2 * TPC])
        w_in = {k: sb("w_in_" + k, [P, P]) for k in "qkvo"}
        rows = sb("rows", [NROWS, P])
        rows_h = sb("rows_h", [NROWS, P])
        qw_in = sb("qw_in", [P, NLIN, P], I32)
        qs_in = sb("qs_in", [P, NLIN, NSC])
        la_in = [sb("la_in0", [P, P]), sb("la_in1", [2 * RANK, P])]
        lb_in = sb("lb_in", [P, NLIN, RANK])
        w_t = {k: sb("w_t_" + k, [P, P]) for k in "qkv"}
        wo_split = sb("wo_split", [P, 2, 2, P])
        wo_t = sb("wo_t", [P, 2, 2, P])
        cols = sb("cols", [P, NROWS])
        cols_h = sb("cols_h", [P, NROWS])
        row_mid = sb("row_mid", [NROWS, P], BF16)
        row_r1 = sb("row_r1", [NROWS, P])
        row_r2 = sb("row_r2", [NROWS, P])
        bias3 = sb("bias3", [P, P], BF16)
        pick = sb("pick", [P, NROWS], BF16)
        pick_a = sb("pick_a", [P, NROWS])
        pick_row = sb("pick_row", [P, len(BIAS_ROWS), P], BF16)
        w_deq = sb("w_deq", [P, NLIN, P])
        w_eff = sb("w_eff", [P, NLIN, P])
        lb_t = [sb("lb_t0", [P, P]), sb("lb_t1", [2 * RANK, P])]
        lin_t = sb("lin_t", [P, NLIN, P])
        x_all = sb("x_all", [P, NCHUNK, TPC, D])
        ctx_sb = [sb(f"ctx_sb{i}", [P, TPC, D]) for i in range(2)]
        stats = sb("stats", [P, TPC, 6])
        agg = sb("agg", [P, 4, TPC])
        negmean = sb("negmean", [P, TPC])
        veps = sb("veps", [P, TPC])
        rstd = sb("rstd", [P, TPC])
        nmr = sb("nmr", [P, TPC])
        xln = sb("xln", [P, TPC, D])
        xln_t = sb("xln_t", [P, CHUNK])
        ctx_tr = [sb(f"ctx_tr{i}", [P, CHUNK]) for i in range(2)]
        parts = [sb(f"parts{i}", [P, 2, 2, CHUNK], F16) for i in range(2)]
        k_stack = [sb(f"k_stack{i}", [P, GROUPS, CHUNK], F16) for i in range(2)]
        q_stack = [sb(f"q_stack{i}", [P, GROUPS, SLOTS, CHUNK], F16) for i in range(2)]
        v_diag = [sb(f"v_diag{i}", [P, PPC * HEADS * 32]) for i in range(2)]
        negmax = [sb(f"negmax{i}", [P, SEQ], BF16) for i in range(2)]
        probs = [sb(f"probs{i}", [P, HEADS, SEQ]) for i in range(4)]
        zsum = [sb(f"zsum{i}", [P, SEQ]) for i in range(2)]
        rz = [sb(f"rz{i}", [P, SEQ]) for i in range(2)]
        att_t = [sb(f"att_t{i}", [P, 2, CHUNK // 2]) for i in range(2)]
        st2 = [sb(f"st2_{i}", [P, 2 * TPC, 6]) for i in range(2)]
        ag2 = [sb(f"ag2_{i}", [P, 4, 2 * TPC]) for i in range(2)]
        ve2 = [sb(f"ve2_{i}", [P, 2 * TPC]) for i in range(2)]
        nm2 = [sb(f"nm2_{i}", [P, 2 * TPC]) for i in range(2)]
        rs2 = [sb(f"rs2_{i}", [P, 2 * TPC]) for i in range(2)]
        nmr2 = [sb(f"nmr2_{i}", [P, 2 * TPC]) for i in range(2)]
        z = [[sb(f"z{v}_{i}", [P, TPC, D]) for i in range(2 if v == 0 else 1)] for v in range(4)]
        h = [[sb(f"h{v}_{i}", [P, CHUNK]) for i in range(2 if v < 3 else 1)] for v in range(4)]
        g = [sb(f"g{i}", [P, CHUNK]) for i in range(3)]

        score_ps = [ps(f"score_ps{i}", [P, HEADS * SEQ]) for i in range(2)]
        att_ps = ps("att_ps", [P, CHUNK])
        wo_ps = ps("wo_ps", [P, CHUNK])
        work0 = ps("work0", [P, CHUNK])
        work1 = ps("work1", [P, CHUNK])
        bank = [score_ps[0][:, 0:CHUNK], score_ps[0][:, CHUNK:], score_ps[1][:, 0:CHUNK], score_ps[1][:, CHUNK:],
                att_ps[:, :], wo_ps[:, :], work0[:, :], work1[:, :]]

        s_wload = sem("s_wload")
        s_fload = sem("s_fload")
        s_const = sem("s_const")
        s_cast = sem("s_cast")
        s_wperm = sem("s_wperm")
        s_split = sem("s_split")
        s_tr = sem("s_tr")
        s_wready = sem("s_wready")
        s_pick = sem("s_pick")
        s_deq = sem("s_deq")
        s_lbt_ps = sem("s_lbt_ps")
        s_lbt = sem("s_lbt")
        s_lora = sem("s_lora")
        s_weff = sem("s_weff")
        s_lint_ps = sem("s_lint_ps")
        s_lint = sem("s_lint")
        s_xin = [sem(f"s_xin{i}") for i in range(3)]
        s_ctxin = [sem(f"s_ctxin{i}") for i in range(2)]
        s_aggr = sem("s_aggr")
        s_bn = sem("s_bn")
        s_stats = sem("s_stats")
        s_rstd = sem("s_rstd")
        s_nmr = sem("s_nmr")
        s_xln = sem("s_xln")
        s_xln_ps = sem("s_xln_ps")
        s_xln_t = sem("s_xln_t")
        s_ctx_ps = sem("s_ctx_ps")
        s_ctx_t = sem("s_ctx_t")
        s_q_ps, s_k_ps = sem("s_q_ps"), sem("s_k_ps")
        s_q_hi, s_k_hi = sem("s_q_hi"), sem("s_k_hi")
        s_q_rest, s_k_rest = sem("s_q_rest"), sem("s_k_rest")
        s_q_lo, s_k_lo = sem("s_q_lo"), sem("s_k_lo")
        s_q_out, s_k_out = sem("s_q_out"), sem("s_k_out")
        s_stack = [sem(f"s_stack{i}") for i in range(2)]
        s_v_ps = sem("s_v_ps")
        s_v = sem("s_v")
        s_att_t = sem("s_att_t")
        s_wo = sem("s_wo")
        s_x2 = sem("s_x2")
        s_scores = sem("s_scores")
        s_negmax = sem("s_negmax")
        s_shifted = sem("s_shifted")
        s_exp = sem("s_exp")
        s_zsum = sem("s_zsum")
        s_rz = sem("s_rz")
        s_probs = sem("s_probs")
        s_pv = sem("s_pv")
        p_bn, p_mv, p_st, p_rs, p_nmr = ([sem(f"p_{w}{b}") for b in range(2)] for w in ("bn", "mv", "st", "rs", "nmr"))
        p_z0 = sem("p_z0_scaled")
        p_z = [sem(f"p_z{v}") for v in range(4)]
        p_zt = [sem(f"p_zt{v}") for v in range(4)]
        p_h = [sem(f"p_h{v}") for v in range(4)]
        p_g = [sem(f"p_g{v}") for v in range(4)]
        p_y = [sem(f"p_y{v}") for v in range(4)]
        p_c = [sem(f"p_c{v}") for v in range(4)]
        p_ht = sem("p_ht")
        p_out = sem("p_out")
        s_store = sem("s_store")

        def live(c):
            return not isinstance(c, int) or 0 <= c < NCHUNK

        def some(count):
            return not isinstance(count, int) or count > 0

        def query0(pair, b):
            return 256 * (pair // 2) + SEQ * (pair % 2) + TILE * b

        def chunks(eng, body):
            for c in range(-3, 2):
                body(c, c % 2, c // 2)
            with eng.Fori(1, 6) as i:
                body(2 * i, 0, i)
                body(2 * i + 1, 1, i)
            for c in range(12, NCHUNK + 2):
                body(c, c % 2, c // 2)

        def steps(eng, body):
            for t in range(0, 8):
                body(t, t % 2)
            with eng.Fori(4, 8) as i:
                body(2 * i, 0)
                body(2 * i + 1, 1)
            for t in range(16, NCHUNK + STAGES - 1):
                body(t, t % 2)

        block = es.enter_context(nc.Block())

        @block.sync
        def _(sp):
            for k, src in (("q", wq), ("k", wk)):
                sp.dma_start(w_in[k][:, :], src).then_inc(s_wload, 16)
            for r, src in ((ROW_BQ, bq), (ROW_BK, bk), (ROW_BV, bv), (ROW_BO, bo)):
                sp.dma_start(rows[r:r + 1, :], src.rearrange("(a n) -> a n", a=1)).then_inc(s_wload, 16)
            sp.dma_start(rows[ROW_BL:ROW_BL + NLIN, :], qb).then_inc(s_wload, 16)
            sp.dma_start(rows[ROW_GAMMA:ROW_GAMMA + NBLK, :], gamma).then_inc(s_wload, 16)
            sp.dma_start(rows[ROW_BETA:ROW_BETA + NBLK, :], beta).then_inc(s_wload, 16)
            for k, src in (("v", wv), ("o", wo)):
                sp.dma_start(w_in[k][:, :], src).then_inc(s_wload, 16)

            def chunk(c, par, half):
                if isinstance(c, int) and c == -2:
                    sp.dma_start(x_all[:, 2:, :, :], x_pt[:, 2:, :, :]).then_inc(s_xin[2], 16)
                    sp.dma_start(qw_in[:, :, :], qw.rearrange("l o d -> o l d")).then_inc(s_fload, 16)
                    sp.dma_start(qs_in[:, :, :], qs.rearrange("l o s -> o l s")).then_inc(s_fload, 16)
                    la_rows = la.rearrange("l r d -> (l r) d")
                    sp.dma_start(la_in[0][:, :], la_rows[0:P, :]).then_inc(s_fload, 16)
                    sp.dma_start(la_in[1][:, :], la_rows[P:, :]).then_inc(s_fload, 16)
                    sp.dma_start(lb_in[:, :, :], lb.rearrange("l o r -> o l r")).then_inc(s_fload, 16)
                if live(c + 4):
                    if live(c + 2):
                        sp.wait_ge(s_ctx_ps, c + 3)
                    sp.dma_start(ctx_sb[par][:, :, :], ctx_t[c + 4]).then_inc(s_ctxin[par], 16)
                if live(c + 2):
                    sp.wait_ge(s_q_lo, c + 3)
                    sp.dma_start(parts_dram[c + 2, 0].rearrange("l f t -> f l t"),
                                 parts[par][:, 0, :, :]).then_inc(s_q_out, 16)
                    if live(c):
                        sp.wait_ge(s_scores, PPC * (c + 1))
                    sp.wait_ge(s_k_lo, c + 3)
                    sp.dma_start(parts_dram[c + 2, 1].rearrange("l f t -> f l t"),
                                 parts[par][:, 1, :, :]).then_inc(s_k_out, 16)
                    sp.wait_ge(s_q_out, 16 * (c + 3))
                    for t in range(TERMS):
                        src = parts_dram[c + 2, 0, t % 2].rearrange("(g s j) t -> s j g t", g=GROUPS, s=SLOTS)
                        for s in range(SLOTS):
                            r = 32 * t + DH * s
                            sp.dma_start(q_stack[par][r:r + DH, :, s, :], src[s]).then_inc(s_stack[par], 16)
                    sp.wait_ge(s_k_out, 16 * (c + 3))
                    for t in range(TERMS):
                        sp.dma_start(k_stack[par][32 * t:32 * t + 32, :, :],
                                     parts_dram[c + 2, 1, t // 2].rearrange("(g r) t -> r g t", g=GROUPS)
                                     ).then_inc(s_stack[par], 16)

            sp.dma_start(x_all[:, 0, :, :], x_t[0]).then_inc(s_xin[0], 16)
            sp.dma_start(ctx_sb[0][:, :, :], ctx_t[0]).then_inc(s_ctxin[0], 16)
            sp.dma_start(x_all[:, 1, :, :], x_t[1]).then_inc(s_xin[1], 16)
            chunks(sp, chunk)

            def step(t, par):
                k = t - 7
                if live(k):
                    sp.wait_ge(p_out, k + 1)
                    sp.dma_start(out_t[k], x_all[:, k, :, :]).then_inc(s_store, 16)

            steps(sp, step)
            sp.wait_ge(s_store, 16 * NCHUNK)

        @block.gpsimd
        def _(pool):
            nc.gpsimd.memset(ident[:, :], 0.0).then_inc(s_const, 1)
            pool.wait_ge(s_const, 1)
            nc.gpsimd.affine_select(out=ident[:, :], in_=ident[:, :], compare_op=ALU.not_equal, fill=1.0, base=0,
                                    pattern=[[-1, P]], channel_multiplier=1).then_inc(s_const, 1)
            nc.gpsimd.memset(minus_half[:, :], -0.5).then_inc(s_const, 1)
            nc.gpsimd.memset(bias3[:, :], 0.0).then_inc(s_const, 1)
            nc.gpsimd.memset(wo_split[:, :, :, :], 0.0).then_inc(s_const, 1)
            for i in range(2):
                nc.gpsimd.memset(q_stack[i][:, :, :, :].bitcast(F32), 0.0).then_inc(s_const, 1)
            for i in range(2):
                nc.gpsimd.memset(v_diag[i][:, :], 0.0).then_inc(s_const, 1)

            def chunk(c, par, half):
                for p in range(PPC):
                    n = PPC * c + p
                    mc = c - (p == 0)
                    if live(mc):
                        m = n - 1
                        pool.wait_ge(s_rz, m + 1)
                        e = probs[(p - 1) % 4]
                        nc.gpsimd.tensor_tensor(e[:, :, :], e[:, :, :],
                                                rz[(p - 1) % 2][:, :].unsqueeze(1).broadcast_to([P, HEADS, SEQ]),
                                                ALU.mult).then_inc(s_probs, 1)
                    if p == 1 and live(c + 3):
                        pool.wait_ge(s_stats, c + 4)
                        if some(c + 3):
                            pool.wait_ge(s_nmr, c + 3)
                            pool.wait_ge(s_xln, c + 3)
                        nc.gpsimd.tensor_tensor(rstd[:, :], veps[:, :], minus_half[:, 0:TPC], ALU.pow).then_inc(s_rstd, 1)

            chunks(pool, chunk)

            def norm_scales(b, lo, hi, count):
                pool.wait_ge(p_st[b], count)
                nc.gpsimd.tensor_tensor(rs2[b][:, lo:hi], ve2[b][:, lo:hi], minus_half[:, lo:hi],
                                        ALU.pow).then_inc(p_rs[b], 1)
                pool.wait_ge(p_rs[b], count)
                nc.gpsimd.tensor_tensor(nmr2[b][:, lo:hi], nm2[b][:, lo:hi], rs2[b][:, lo:hi],
                                        ALU.mult).then_inc(p_nmr[b], 1)

            def step(t, par):
                if live(t) or live(t - 6):
                    if live(t - 7):
                        pool.wait_ge(p_z[3], t - 6)
                    norm_scales(0, 0 if live(t) else TPC, 2 * TPC if live(t - 6) else TPC, t + 1)
                if live(t - 4) or live(t - 2):
                    if live(t - 5):
                        pool.wait_ge(p_z[2], t - 4)
                    if live(t - 3):
                        pool.wait_ge(p_z[1], t - 2)
                    norm_scales(1, 0 if live(t - 4) else TPC, 2 * TPC if live(t - 2) else TPC, t - 1)
                if live(t):
                    if some(t - 1):
                        pool.wait_ge(p_zt[0], t - 1)
                    nc.gpsimd.tensor_tensor(z[0][par][:, :, :], x_all[:, t, :, :],
                                            rs2[0][:, 0:TPC].unsqueeze(2).broadcast_to([P, TPC, D]),
                                            ALU.mult).then_inc(p_z0, 1)
                    pool.wait_ge(p_nmr[0], t + 1)
                    pool.wait_ge(p_z0, t + 1)
                    nc.gpsimd.tensor_tensor(z[0][par][:, :, :], z[0][par][:, :, :],
                                            nmr2[0][:, 0:TPC].unsqueeze(2).broadcast_to([P, TPC, D]),
                                            ALU.add).then_inc(p_z[0], 1)

            steps(pool, step)

        @block.vector
        def _(dve):
            dve.wait_ge(s_const, 2)
            nc.vector.tensor_copy(ident_bf[:, :], ident[:, :]).then_inc(s_cast, 1)
            nc.vector.tensor_scalar(neg_ident[:, :], ident[:, :], -1.0, None, ALU.mult).then_inc(s_cast, 1)
            nc.vector.tensor_tensor(pick_a[:, :], ident[:, 0:NROWS], ident[:, 32:32 + NROWS], ALU.add).then_inc(s_pick, 1)
            dve.wait_ge(s_pick, 1)
            nc.vector.tensor_tensor(pick[:, :], pick_a[:, :], ident[:, 64:64 + NROWS], ALU.add).then_inc(s_pick, 1)
            dve.wait_ge(s_pick, 2)
            for i, r in enumerate(BIAS_ROWS):
                nc.vector.tensor_copy(pick_row[:, i, :], pick[:, r:r + 1].broadcast_to([P, P])).then_inc(s_pick, 1)
            dve.wait_ge(s_wload, 16 * 11)
            dve.wait_ge(s_const, 5)
            wo_cols = w_in["o"][:, :].rearrange("p (j o u) -> p o u j", o=2, u=8)
            for o in range(2):
                for b in range(2):
                    dst = wo_split[:, o, b, :].rearrange("p (u b j) -> p b u j", u=8, b=2)
                    nc.vector.tensor_copy(dst[:, b], wo_cols[:, o]).then_inc(s_wperm, 1)
            nc.vector.tensor_copy(rows_h[:, :].rearrange("p (h j) -> p h j", j=DH),
                                  rows[:, :].rearrange("p (j h) -> p h j", j=DH)).then_inc(s_wperm, 1)
            nc.vector.tensor_copy(bias3[0:NROWS, :], rows[:, :]).then_inc(s_split, 1)
            dve.wait_ge(s_split, 1)
            nc.vector.tensor_tensor(row_r1[:, :], rows[:, :], bias3[0:NROWS, :], ALU.subtract).then_inc(s_split, 1)
            dve.wait_ge(s_split, 2)
            nc.vector.tensor_copy(bias3[32:32 + NROWS, :], row_r1[:, :]).then_inc(s_split, 1)
            nc.vector.tensor_copy(row_mid[:, :], row_r1[:, :]).then_inc(s_split, 1)
            dve.wait_ge(s_split, 4)
            nc.vector.tensor_tensor(row_r2[:, :], row_r1[:, :], row_mid[:, :],
                                    ALU.subtract).then_inc(s_split, 1)
            dve.wait_ge(s_split, 5)
            nc.vector.tensor_copy(bias3[64:64 + NROWS, :], row_r2[:, :]).then_inc(s_split, 1)

            def feed_forward_weights():
                dve.wait_ge(s_fload, 16 * 5)
                nc.vector.tensor_scalar(w_deq[:, :, :], qw_in[:, :, :], 1.0 / 7.5, -1.0, ALU.mult,
                                        ALU.add).then_inc(s_deq, 1)
                dve.wait_ge(s_deq, 1)
                nc.vector.tensor_tensor(
                    w_deq[:, :, :].rearrange("p l (s e) -> p (l s) e", e=GROUP),
                    w_deq[:, :, :].rearrange("p l (s e) -> p (l s) e", e=GROUP),
                    qs_in[:, :, :].rearrange("p l s -> p (l s)").unsqueeze(2).broadcast_to([P, NLIN * NSC, GROUP]),
                    ALU.mult).then_inc(s_deq, 1)
                dve.wait_ge(s_lbt_ps, 2)
                nc.vector.tensor_copy(lb_t[0][:, :], bank[4][:, 0:P]).then_inc(s_lbt, 1)
                nc.vector.tensor_copy(lb_t[1][:, :], bank[5][0:2 * RANK, 0:P]).then_inc(s_lbt, 1)
                dve.wait_ge(s_deq, 2)
                for i in range(NLIN):
                    dve.wait_ge(s_lora, i + 1)
                    nc.vector.tensor_tensor(w_eff[:, i, :], bank[i % 4][:, 0:P] if i < 4 else bank[i][:, 0:P],
                                            w_deq[:, i, :], ALU.add).then_inc(s_weff, 1)

            def combine(k, bn_done, step_done, used, done, st, ag, ve, nm):
                dve.wait_ge(bn_done, k + 1)
                nc.vector.tensor_tensor(ag[:, 0, :], st[:, :, 1], st[:, :, 4], ALU.add)
                nc.vector.scalar_tensor_tensor(ag[:, 1, :], st[:, :, 2], EPS * D, st[:, :, 5], ALU.add, ALU.add)
                nc.vector.tensor_tensor(ag[:, 2, :], st[:, :, 1], st[:, :, 4], ALU.subtract).then_inc(step_done, 1)
                dve.wait_ge(step_done, 2 * k + 1)
                nc.vector.scalar_tensor_tensor(ag[:, 3, :], ag[:, 2, :], 0.25, ag[:, 2, :], ALU.mult,
                                               ALU.mult).then_inc(step_done, 1)
                dve.wait_ge(step_done, 2 * k + 2)
                if some(k):
                    dve.wait_ge(used, k)
                nc.vector.tensor_scalar(nm[:, :], ag[:, 0, :], -0.5, None, ALU.mult)
                nc.vector.scalar_tensor_tensor(ve[:, :], ag[:, 1, :], 1.0 / D, ag[:, 3, :], ALU.mult,
                                               ALU.add).then_inc(done, 1)

            def chunk(c, par, half):
                if isinstance(c, int) and c == -1:
                    feed_forward_weights()
                for p in range(PPC):
                    n = PPC * c + p
                    if live(c):
                        dve.wait_ge(s_scores, n + 1)
                        if some(n - 1):
                            dve.wait_ge(s_shifted, n - 1)
                        nc.vector.tensor_reduce(negmax[p % 2][:, :],
                                                score_ps[p % 2][:, :].rearrange("p (h k) -> p k h", k=SEQ),
                                                AX_X, ALU.max, negate=True).then_inc(s_negmax, 1)
                    if p == 3 and live(c - 2):
                        dve.wait_ge(s_wo, c - 1)
                        nc.vector.tensor_tensor(x_all[:, c - 2, :, :],
                                                wo_ps[:, :].rearrange("p (t d) -> p t d", t=TPC),
                                                x_all[:, c - 2, :, :], ALU.add).then_inc(s_x2, 1)
                    if p == 1 and live(c + 3):
                        if isinstance(c, int) and c + 3 < 3:
                            dve.wait_ge(s_xin[c + 3], 16)
                        for t in range(TPC):
                            ins = nc.vector.bn_stats(stats[:, t, :], x_all[:, c + 3, t, :])
                        ins.then_inc(s_bn, 1)
                        combine(c + 3, s_bn, s_aggr, s_nmr, s_stats, stats, agg, veps, negmean)
                    mc = c - (p == 0)
                    if live(mc):
                        m = n - 1
                        q = (p - 1) % 2
                        dve.wait_ge(s_exp, m + 1)
                        nc.vector.tensor_reduce(zsum[q][:, :], probs[(p - 1) % 4][:, :, :].rearrange("p h k -> p k h"),
                                                AX_X, ALU.add).then_inc(s_zsum, 1)
                        dve.wait_ge(s_zsum, m + 1)
                        if some(m - 1):
                            dve.wait_ge(s_probs, m - 1)
                        nc.vector.reciprocal(rz[q][:, :], zsum[q][:, :]).then_inc(s_rz, 1)
                    if p == 2 and live(c + 3):
                        dve.wait_ge(s_rstd, c + 4)
                        if some(c + 3):
                            dve.wait_ge(s_xln, c + 3)
                        nc.vector.tensor_tensor(nmr[:, :], negmean[:, :], rstd[:, :], ALU.mult).then_inc(s_nmr, 1)

            chunks(dve, chunk)

            def batch_stats(b, lo, hi, count):
                combine(count - 1, p_bn[b], p_mv[b], p_nmr[b], p_st[b], st2[b][:, lo:hi, :], ag2[b][:, :, lo:hi],
                        ve2[b][:, lo:hi], nm2[b][:, lo:hi])

            def step(t, par):
                if isinstance(t, int) and t == 0:
                    dve.wait_ge(s_x2, NCHUNK)
                if live(t):
                    for i in range(TPC):
                        ins = nc.vector.bn_stats(st2[0][:, i, :], x_all[:, t, i, :])
                if live(t - 6):
                    dve.wait_ge(p_y[3], t - 5)
                    for i in range(TPC):
                        ins = nc.vector.bn_stats(st2[0][:, TPC + i, :], bank[0][:, TILE * i:TILE * (i + 1)])
                if live(t) or live(t - 6):
                    ins.then_inc(p_bn[0], 1)
                    batch_stats(0, 0 if live(t) else TPC, 2 * TPC if live(t - 6) else TPC, t + 1)
                if live(t - 4):
                    dve.wait_ge(p_y[2], t - 3)
                    for i in range(TPC):
                        ins = nc.vector.bn_stats(st2[1][:, i, :], bank[1][:, TILE * i:TILE * (i + 1)])
                if live(t - 2):
                    dve.wait_ge(p_y[1], t - 1)
                    for i in range(TPC):
                        ins = nc.vector.bn_stats(st2[1][:, TPC + i, :], bank[2][:, TILE * i:TILE * (i + 1)])
                if live(t - 4) or live(t - 2):
                    ins.then_inc(p_bn[1], 1)
                    batch_stats(1, 0 if live(t - 4) else TPC, 2 * TPC if live(t - 2) else TPC, t - 1)
                for v, k, src in ((3, t - 7, bank[6]), (2, t - 5, bank[3]), (1, t - 3, bank[4])):
                    if live(k):
                        q = (par - 2 * v - 1) % 2
                        dve.wait_ge(p_c[v], k + 1)
                        if v == 3:
                            if some(k):
                                dve.wait_ge(p_ht, k)
                        elif some(k - 1):
                            dve.wait_ge(p_h[v + 1], k - 1)
                        nc.vector.scalar_tensor_tensor(h[v][0 if v == 3 else q][:, :], src,
                                                       cols[:, ROW_BL + 2 * v - 1:ROW_BL + 2 * v],
                                                       h[v - 1][q][:, :], ALU.add, ALU.add).then_inc(p_h[v], 1)
                if live(t - 7):
                    k = t - 7
                    dve.wait_ge(p_ht, k + 1)
                    nc.vector.tensor_tensor(x_all[:, k, :, :], bank[5].rearrange("p (t d) -> p t d", t=TPC),
                                            x_all[:, k, :, :], ALU.add).then_inc(p_out, 1)

            steps(dve, step)

        @block.scalar
        def _(act):
            for i, k in enumerate("qkv"):
                act.wait_ge(s_tr, i + 1)
                nc.scalar.activation(w_t[k][:, :].rearrange("p (h j) -> p h j", j=DH),
                                     bank[i][:, 0:P].rearrange("p (j h) -> p h j", j=DH), ACT.Copy).then_inc(s_wready, 1)
            act.wait_ge(s_tr, 4)
            nc.scalar.activation(cols[:, :], bank[3][:, 0:NROWS], ACT.Copy).then_inc(s_wready, 1)
            nc.scalar.activation(cols_h[:, :], bank[3][:, NROWS:2 * NROWS], ACT.Copy).then_inc(s_wready, 1)
            act.wait_ge(s_tr, 5)
            nc.scalar.activation(wo_t[:, :, :, :].rearrange("p o b n -> p (o b n)"), bank[4], ACT.Copy).then_inc(s_wready, 1)

            act.wait_ge(s_wready, 6)

            def feed_forward_weights():
                for i in range(NLIN):
                    act.wait_ge(s_lint_ps, i + 1)
                    nc.scalar.activation(lin_t[:, i, :], bank[i][:, 0:P] if i < 4 else bank[i % 4][:, P:2 * P],
                                         ACT.Copy).then_inc(s_lint, 1)

            def chunk(c, par, half):
                if isinstance(c, int) and c == -1:
                    feed_forward_weights()

                def exponentials(p):
                    n = PPC * c + p
                    act.wait_ge(s_shifted, n + 1)
                    if some(n - 3):
                        act.wait_ge(s_pv, n - 3)
                    nc.scalar.activation(probs[p][:, :, :].rearrange("p h k -> p (h k)"), score_ps[p % 2][:, :],
                                         ACT.Exp, scale=SCALE).then_inc(s_exp, 1)

                if live(c + 2):
                    act.wait_ge(s_xln_ps, c + 3)
                    if some(c + 2):
                        act.wait_ge(s_q_ps, c + 2)
                    nc.scalar.activation(xln_t[:, :], work0[:, :], ACT.Copy).then_inc(s_xln_t, 1)
                if live(c):
                    exponentials(0)
                if live(c + 2):
                    act.wait_ge(s_ctx_ps, c + 3)
                    if some(c + 1):
                        act.wait_ge(s_v_ps, c + 1)
                    nc.scalar.activation(ctx_tr[par][:, :], work1[:, :], ACT.Copy).then_inc(s_ctx_t, 1)
                if live(c + 2):
                    act.wait_ge(s_q_ps, c + 3)
                    if some(c + 1):
                        act.wait_ge(s_q_out, 16 * (c + 1))
                    nc.scalar.activation(parts[par][:, 0, 0, :], work0[:, :], ACT.Identity,
                                         bias=cols_h[:, ROW_BQ:ROW_BQ + 1]).then_inc(s_q_hi, 1)
                if live(c):
                    exponentials(1)
                if live(c + 2):
                    act.wait_ge(s_q_rest, c + 3)
                    nc.scalar.activation(parts[par][:, 0, 1, :], work0[:, :], ACT.Identity,
                                         bias=cols_h[:, ROW_BQ:ROW_BQ + 1]).then_inc(s_q_lo, 1)
                if live(c - 1):
                    act.wait_ge(s_pv, PPC * c)
                    if some(c - 2):
                        act.wait_ge(s_wo, c - 2)
                    nc.scalar.activation(att_t[1 - par][:, :, :].rearrange("p o t -> p (o t)"), att_ps[:, :],
                                         ACT.Copy).then_inc(s_att_t, 1)
                if live(c + 2):
                    act.wait_ge(s_k_ps, c + 3)
                    if some(c + 1):
                        act.wait_ge(s_k_out, 16 * (c + 1))
                    nc.scalar.activation(parts[par][:, 1, 0, :], work1[:, :], ACT.Identity,
                                         bias=cols_h[:, ROW_BK:ROW_BK + 1]).then_inc(s_k_hi, 1)
                if live(c):
                    exponentials(2)
                if live(c + 2):
                    act.wait_ge(s_k_rest, c + 3)
                    nc.scalar.activation(parts[par][:, 1, 1, :], work1[:, :], ACT.Identity,
                                         bias=cols_h[:, ROW_BK:ROW_BK + 1]).then_inc(s_k_lo, 1)
                if live(c + 1):
                    act.wait_ge(s_v_ps, c + 2)
                    if live(c - 1):
                        act.wait_ge(s_pv, PPC * c)
                    elif isinstance(c, int) and c == -1:
                        act.wait_ge(s_const, 9)
                    for b in range(2):
                        dst = v_diag[1 - par][SEQ * b:SEQ * (b + 1), :].rearrange("p (u a e) -> p u a e", a=4, e=16)
                        ins = nc.scalar.activation(
                            dst[:, :, 0:4:3, DH * b:DH * (b + 1)],
                            work0[SEQ * b:SEQ * (b + 1), :].rearrange("p (u s j) -> p u s j", s=2, j=DH), ACT.Copy)
                    ins.then_inc(s_v, 1)
                if live(c):
                    exponentials(3)
                if live(c + 3):
                    act.wait_ge(s_nmr, c + 4)
                    act.wait_ge(s_rstd, c + 4)
                    if some(c + 3):
                        act.wait_ge(s_xln_ps, c + 3)
                    for t in range(TPC):
                        ins = nc.scalar.activation(xln[:, t, :], x_all[:, c + 3, t, :], ACT.Identity,
                                                   bias=nmr[:, t:t + 1], scale=rstd[:, t:t + 1])
                    ins.then_inc(s_xln, 1)

            chunks(act, chunk)

            def normalise(v, k, b, lo, count, src):
                act.wait_ge(p_nmr[b], count)
                if some(k):
                    act.wait_ge(p_zt[v], k)
                for t in range(TPC):
                    ins = nc.scalar.activation(z[v][0][:, t, :], src[:, TILE * t:TILE * (t + 1)], ACT.Identity,
                                               bias=nmr2[b][:, lo + t:lo + t + 1], scale=rs2[b][:, lo + t:lo + t + 1])
                ins.then_inc(p_z[v], 1)

            def step(t, par):
                for v, k, src in ((3, t - 7, bank[3]), (2, t - 5, bank[4]), (1, t - 3, bank[5])):
                    if live(k):
                        act.wait_ge(p_zt[v], k + 1)
                        if some(k):
                            act.wait_ge(p_c[v], k)
                        nc.scalar.activation(g[v - 1][:, :], src, ACT.Gelu,
                                             bias=cols[:, ROW_BETA + v - 1:ROW_BETA + v],
                                             scale=cols[:, ROW_GAMMA + v - 1:ROW_GAMMA + v]).then_inc(p_g[v], 1)
                if live(t - 6):
                    normalise(3, t - 6, 0, TPC, t + 1, bank[0])
                if live(t - 4):
                    normalise(2, t - 4, 1, 0, t - 1, bank[1])
                if live(t - 2):
                    normalise(1, t - 2, 1, TPC, t - 1, bank[2])
                if live(t - 1):
                    k = t - 1
                    act.wait_ge(p_zt[0], k + 1)
                    if some(k - 1):
                        act.wait_ge(p_h[1], k - 1)
                    nc.scalar.activation(h[0][(par - 1) % 2][:, :], bank[7], ACT.Copy).then_inc(p_h[0], 1)

            steps(act, step)

        @block.tensor
        def _(pe):
            pe.wait_ge(s_const, 2)
            pe.wait_ge(s_wload, 16 * 11)
            for i, k in enumerate("qkv"):
                nc.tensor.transpose(bank[i][:, 0:P], w_in[k][:, :], ident[:, :]).then_inc(s_tr, 1)
            pe.wait_ge(s_wperm, 5)
            nc.tensor.transpose(bank[3][:, 0:NROWS], rows[:, :], ident[0:NROWS, 0:NROWS])
            nc.tensor.transpose(bank[3][:, NROWS:2 * NROWS], rows_h[:, :],
                                ident[0:NROWS, 0:NROWS]).then_inc(s_tr, 1)
            for o in range(2):
                for b in range(2):
                    ins = nc.tensor.transpose(bank[4][:, P * (2 * o + b):P * (2 * o + b + 1)], wo_split[:, o, b, :],
                                              ident[:, :])
            ins.then_inc(s_tr, 1)
            pe.wait_ge(s_wready, 6)
            pe.wait_ge(s_cast, 2)
            pe.wait_ge(s_pick, 2 + len(BIAS_ROWS))
            pe.wait_ge(s_split, 6)

            def feed_forward_weights():
                pe.wait_ge(s_fload, 16 * 5)
                lb_cols = lb_in[:, :, :].rearrange("p l r -> p (l r)")
                nc.tensor.transpose(bank[4][:, 0:P], lb_cols[:, 0:P], ident[:, :]).then_inc(s_lbt_ps, 1)
                nc.tensor.transpose(bank[5][0:2 * RANK, 0:P], lb_cols[:, P:], ident[:, :]).then_inc(s_lbt_ps, 1)
                pe.wait_ge(s_lbt, 2)
                for i in range(NLIN):
                    r = RANK * (i % 4)
                    nc.tensor.matmul(bank[i][:, 0:P], lb_t[i // 4][r:r + RANK, :], la_in[i // 4][r:r + RANK, :],
                                     start=True, stop=True).then_inc(s_lora, 1)
                for i in range(NLIN):
                    pe.wait_ge(s_weff, i + 1 if i < 4 else NLIN)
                    if i >= 4:
                        pe.wait_ge(s_lint, i - 3)
                    nc.tensor.transpose(bank[i][:, 0:P] if i < 4 else bank[i % 4][:, P:2 * P], w_eff[:, i, :],
                                        ident[:, :]).then_inc(s_lint_ps, 1)

            def bias_rows(dst, which, head_major=False):
                src = bias3[:, :].rearrange("p (j h) -> p h j", j=DH) if head_major else bias3[:, :]
                src = src.unsqueeze(1).broadcast_to([P, TPC] + list(src.shape[1:]))
                nc.tensor.matmul(dst, pick_row[:, which, :], src, start=True, stop=False, skip_group_check=True)

            def project_out(t, att):
                b, u = t % 2, t // 2
                for o in range(2):
                    ins = nc.tensor.matmul(wo_ps[:, TILE * t:TILE * (t + 1)], att[:, o, TILE * u:TILE * (u + 1)],
                                           wo_t[:, o, b, :], start=False, stop=o == 1, skip_group_check=True)
                return ins

            def chunk(c, par, half):
                if isinstance(c, int) and c == -1:
                    feed_forward_weights()
                for p in range(PPC):
                    n = PPC * c + p
                    mc, mp = (c, p + 1) if p < 3 else (c + 1, 0)
                    if live(mc):
                        m = n + 1
                        mpar = mp % 2
                        mb = par if p < 3 else 1 - par
                        if mp == 0:
                            mh = half if par == 0 else half + 1
                            pe.wait_ge(s_stack[mb], 16 * STACK_DMAS * (mh + 1))
                            if isinstance(c, int) and c == -1:
                                pe.wait_ge(s_lint, NLIN)
                        if some(m - 1):
                            pe.wait_ge(s_exp, m - 1)
                        for grp in range(GROUPS):
                            for b in range(2):
                                q0, k0 = query0(mp, b), TILE * mp + SEQ * b
                                ins = nc.tensor.matmul(
                                    score_ps[mpar][SEQ * b:SEQ * (b + 1), 256 * grp:256 * (grp + 1)],
                                    k_stack[mb][:, grp, k0:k0 + SEQ], q_stack[mb][:, grp, :, q0:q0 + SEQ],
                                    start=grp % 2 == 0, stop=False, skip_group_check=True)
                        ins.then_inc(s_scores, 1)
                    if p == 0 and live(c + 2):
                        pe.wait_ge(s_xln, c + 3)
                        if some(c + 1):
                            pe.wait_ge(s_v, c + 1)
                        for t in range(TPC):
                            ins = nc.tensor.transpose(work0[:, TILE * t:TILE * (t + 1)], xln[:, t, :], ident[:, :])
                        ins.then_inc(s_xln_ps, 1)
                    if p == 1 and live(c + 2):
                        pe.wait_ge(s_xln_t, c + 3)
                        nc.tensor.matmul(work0[:, :], w_t["q"][:, :], xln_t[:, :], start=True, stop=False,
                                         skip_group_check=True).then_inc(s_q_ps, 1)
                    if p == 2 and live(c + 2):
                        pe.wait_ge(s_ctx_t, c + 3)
                        nc.tensor.matmul(work1[:, :], w_t["k"][:, :], ctx_tr[par][:, :], start=True, stop=False,
                                         skip_group_check=True).then_inc(s_k_ps, 1)
                    if p == 3 and live(c + 1):
                        if live(c + 2):
                            pe.wait_ge(s_q_lo, c + 3)
                        elif some(c + 1):
                            pe.wait_ge(s_v, c + 1)
                        bias_rows(work0[:, :], 0, head_major=True)
                        for q in range(PPC):
                            ins = nc.tensor.matmul(work0[:, TILE * q:TILE * (q + 1)],
                                                   ctx_tr[1 - par][:, TILE * q:TILE * (q + 1)], w_t["v"][:, :],
                                                   start=False, stop=True, skip_group_check=True)
                        ins.then_inc(s_v_ps, 1)
                    if live(c):
                        pe.wait_ge(s_negmax, n + 1)
                        for o in range(2):
                            ins = nc.tensor.matmul(score_ps[p % 2][:, CHUNK * o:CHUNK * (o + 1)], ident_bf[:, :],
                                                   negmax[p % 2][:, :].unsqueeze(1).broadcast_to([P, 8, SEQ]),
                                                   start=False, stop=True, skip_group_check=True)
                        ins.then_inc(s_shifted, 1)
                    if p == 0 and live(c + 2):
                        pe.wait_ge(s_ctxin[par], 16 * (half + 2))
                        if some(c + 2):
                            pe.wait_ge(s_k_lo, c + 2)
                        dst = work1[:, :].rearrange("p (u v b k) -> p u b v k", u=2, v=2, b=2)
                        for t in range(TPC):
                            ins = nc.tensor.transpose(dst[:, t // 2, t % 2], ctx_sb[par][:, t, :], ident[:, :])
                        ins.then_inc(s_ctx_ps, 1)
                    if p == 1 and live(c + 2):
                        pe.wait_ge(s_q_hi, c + 3)
                        nc.tensor.matmul(work0[:, :], neg_ident[:, :], parts[par][:, 0, 0, :], start=False, stop=True,
                                         skip_group_check=True).then_inc(s_q_rest, 1)
                    if p == 2 and live(c + 2):
                        pe.wait_ge(s_k_hi, c + 3)
                        nc.tensor.matmul(work1[:, :], neg_ident[:, :], parts[par][:, 1, 0, :], start=False, stop=True,
                                         skip_group_check=True).then_inc(s_k_rest, 1)
                    if p == 3 and live(c - 1):
                        pe.wait_ge(s_att_t, c)
                        if some(c - 1):
                            pe.wait_ge(s_x2, c - 1)
                        bias_rows(wo_ps[:, :], 1)
                        project_out(0, att_t[1 - par])
                    if p < 3 and live(c - 2):
                        ins = project_out(p + 1, att_t[par])
                        if p == 2:
                            ins.then_inc(s_wo, 1)
                    mc, mp = (c, p - 2) if p >= 2 else (c - 1, p + 2)
                    if live(mc):
                        m = n - 2
                        mb = par if p >= 2 else 1 - par
                        pe.wait_ge(s_probs, m + 1)
                        if mp == 0:
                            pe.wait_ge(s_v, mc + 1)
                            if some(mc):
                                pe.wait_ge(s_att_t, mc)
                        for o in range(2):
                            for s in range(2):
                                for grp in range(4):
                                    hd = 8 * o + 2 * grp + s
                                    v0 = 32 * (HEADS * mp + hd)
                                    c0 = 256 * o + SEQ * mp
                                    ins = nc.tensor.matmul(
                                        att_ps[32 * grp:32 * (grp + 1), c0:c0 + SEQ], v_diag[mb][:, v0:v0 + 32],
                                        probs[mp][:, hd, :], start=(mp == 0 and o == 0 and s == 0),
                                        stop=False, skip_group_check=True, tile_position=(0, 32 * grp))
                        ins.then_inc(s_pv, 1)
            chunks(pe, chunk)
            pe.wait_ge(s_x2, NCHUNK)

            def transpose_z(v, k, dst, i=0):
                pe.wait_ge(p_z[v], k + 1)
                for t in range(TPC):
                    ins = nc.tensor.transpose(dst[:, TILE * t:TILE * (t + 1)], z[v][i][:, t, :], ident[:, :])
                ins.then_inc(p_zt[v], 1)

            def first_layer(v, hk, dst):
                bias_rows(dst, 1 + v)
                for t in range(TPC):
                    ins = nc.tensor.matmul(dst[:, TILE * t:TILE * (t + 1)], hk[:, TILE * t:TILE * (t + 1)],
                                           lin_t[:, 2 * v - 2, :], start=False, stop=True, skip_group_check=True)
                ins.then_inc(p_y[v], 1)

            def step(t, par):
                for v, k in ((3, t - 6), (2, t - 4), (1, t - 2)):
                    if live(k):
                        pe.wait_ge(p_h[v - 1], k + 1)
                        if some(k):
                            pe.wait_ge(p_z[v], k)
                        first_layer(v, h[v - 1][(par - 2 * v) % 2], bank[3 - v])
                if live(t - 7):
                    if live(t - 6):
                        pe.wait_ge(p_h[2], t - 5)
                    transpose_z(3, t - 7, bank[3])
                if live(t - 5):
                    if live(t - 4):
                        pe.wait_ge(p_h[1], t - 3)
                    transpose_z(2, t - 5, bank[4])
                if live(t - 3):
                    if live(t - 8):
                        pe.wait_ge(p_out, t - 7)
                    transpose_z(1, t - 3, bank[5])
                if live(t - 1):
                    if some(t - 1):
                        pe.wait_ge(p_h[0], t - 1)
                    transpose_z(0, t - 1, bank[7], 1 - par)
                for v, k, dst in ((3, t - 7, bank[6]), (2, t - 5, bank[3]), (1, t - 3, bank[4])):
                    if live(k):
                        pe.wait_ge(p_g[v], k + 1)
                        if some(k):
                            pe.wait_ge(p_h[v], k)
                        nc.tensor.matmul(dst, lin_t[:, 2 * v - 1, :], g[v - 1][:, :], start=True,
                                         stop=True).then_inc(p_c[v], 1)
                if live(t - 7):
                    pe.wait_ge(p_h[3], t - 6)
                    if live(t - 8):
                        pe.wait_ge(p_out, t - 7)
                    for i in range(TPC):
                        ins = nc.tensor.transpose(bank[5][:, TILE * i:TILE * (i + 1)],
                                                  h[3][0][:, TILE * i:TILE * (i + 1)], ident[:, :])
                    ins.then_inc(p_ht, 1)

            steps(pe, step)


_INS = ["x", "ctx_1024", "L0_xattn_Wk_w", "L0_xattn_Wk_b", "L0_xattn_Wq_w", "L0_xattn_Wq_b", "L0_xattn_Wv_w",
        "L0_xattn_Wv_b", "L0_xattn_Wo_w", "L0_xattn_Wo_b", "L0_ffn_qweights", "L0_ffn_scales", "L0_ffn_biases",
        "L0_ffn_lora_a", "L0_ffn_lora_b", "L0_ffn_ln_gamma", "L0_ffn_ln_beta"]


def kernel(**inputs):
    import numpy as _np
    import concourse.bacc as _bacc
    from concourse import mybir as _mybir
    from concourse.bass_utils import run_bass_kernel_spmd as _run

    nc = _bacc.Bacc("TRN2", target_bir_lowering=False, num_devices=1)
    arrays, args = {}, []
    for name in _INS:
        a = _np.ascontiguousarray(inputs[name])
        arrays[f"in_{name}"] = a
        args.append(nc.dram_tensor(f"in_{name}", a.shape, _mybir.dt.from_np(a.dtype), kind="ExternalInput").ap())
    args.append(nc.dram_tensor("out_0", (BATCH, SEQ, D), F32, kind="ExternalOutput").ap())
    build(nc, *args)
    r = _run(nc, [arrays], core_ids=[0])
    return r.results[0]["out_0"]
```

```python
from contextlib import ExitStack

import concourse.bass as bass
from concourse import mybir

F32 = mybir.dt.float32
F16 = mybir.dt.float16
BF16 = mybir.dt.bfloat16
I32 = mybir.dt.int32
ALU = mybir.AluOpType
ACT = mybir.ActivationFunctionType
AX_X = mybir.AxisListType.X

BATCH, SEQ, D = 128, 64, 128
HEADS = 16
DH = D // HEADS
TOKENS = BATCH * SEQ
P = 128
TILE = P
CHUNK = 512
TPC = CHUNK // TILE
NCHUNK = TOKENS // CHUNK
PPC = CHUNK // (2 * SEQ)
GROUPS = 4
SLOTS = HEADS // GROUPS
ROWS_PER_SLOT = DH * 2 * 2
GROUP = 16
NSC = D // GROUP
RANK = 32
NLIN = 6
NBLK = 3
EPS = 1e-5
SCALE = 1.0 / (DH ** 0.5)
STACK_DMAS = SLOTS + 2

ROW_BQ, ROW_BK, ROW_BV, ROW_BO = 0, 1, 2, 3
ROW_BL = 4
ROW_GAMMA = ROW_BL + NLIN
ROW_BETA = ROW_GAMMA + NBLK
NROWS = ROW_BETA + NBLK
BIAS_ROWS = [ROW_BV, ROW_BO, ROW_BL, ROW_BL + 2, ROW_BL + 4]

STAGES = 8
EARLY = {0: (12, 3), 1: (13, 3), 2: (15, 0), 3: (16, 0), 4: (16, 2)}
FIRST_STEP = 5


def build(nc, x, ctx_in, wk, bk, wq, bq, wv, bv, wo, bo, qw, qs, qb, la, lb, gamma, beta, out):
    x_t = x.rearrange("b s d -> (b s) d").rearrange("(c t p) d -> c p t d", t=TPC, p=P)
    ctx_t = ctx_in.rearrange("b s d -> (b s) d").rearrange("(c t p) d -> c p t d", t=TPC, p=P)
    out_t = out.rearrange("b s d -> (b s) d").rearrange("(c t p) d -> c p t d", t=TPC, p=P)
    x_pt = x.rearrange("b s d -> (b s) d").rearrange("(c t p) d -> p c t d", t=TPC, p=P)
    q_dram = nc.dram_tensor("q_parts", [NCHUNK, P, 2, 2 * CHUNK], F16, kind="Internal").ap()
    k_dram = nc.dram_tensor("k_parts", [NCHUNK, P, 2, CHUNK], F16, kind="Internal").ap()

    with ExitStack() as es:
        def sb(name, shape, dt=F32):
            return es.enter_context(nc.sbuf_tensor(name, shape, dt))

        def ps(name, shape, dt=F32):
            return es.enter_context(nc.psum_tensor(name, shape, dt))

        def sem(name):
            return es.enter_context(nc.semaphore(name))

        ident = sb("ident", [P, P])
        ident_bf = sb("ident_bf", [P, P], BF16)
        neg_ident = sb("neg_ident", [P, P], F16)
        minus_half = sb("minus_half", [P, 2 * TPC])
        w_in = {k: sb("w_in_" + k, [P, P]) for k in "qkvo"}
        rows = sb("rows", [NROWS, P])
        rows_h = sb("rows_h", [NROWS, P])
        qw_in = sb("qw_in", [P, NLIN, P], I32)
        qs_in = sb("qs_in", [P, NLIN, NSC])
        la_in = [sb("la_in0", [P, P]), sb("la_in1", [2 * RANK, P])]
        lb_in = sb("lb_in", [P, NLIN, RANK])
        w_t = {k: sb("w_t_" + k, [P, P]) for k in "qkv"}
        wo_split = sb("wo_split", [P, 2, 2, P])
        wo_t = sb("wo_t", [P, 2, 2, P])
        cols = sb("cols", [P, NROWS])
        cols_h = sb("cols_h", [P, NROWS])
        row_mid = sb("row_mid", [NROWS, P], BF16)
        row_r1 = sb("row_r1", [NROWS, P])
        row_r2 = sb("row_r2", [NROWS, P])
        bias3 = sb("bias3", [P, P], BF16)
        pick = sb("pick", [P, NROWS], BF16)
        pick_a = sb("pick_a", [P, NROWS])
        pick_row = sb("pick_row", [P, len(BIAS_ROWS), P], BF16)
        w_deq = sb("w_deq", [P, NLIN, P])
        w_eff = sb("w_eff", [P, NLIN, P])
        lb_t = [sb("lb_t0", [P, P]), sb("lb_t1", [2 * RANK, P])]
        lin_t = sb("lin_t", [P, NLIN, P])
        x_all = sb("x_all", [P, NCHUNK, TPC, D])
        ctx_sb = [sb(f"ctx_sb{i}", [P, TPC, D]) for i in range(2)]
        stats = sb("stats", [P, TPC, 6])
        agg = sb("agg", [P, 4, TPC])
        neg2mean = sb("neg2mean", [P, TPC])
        veps4 = sb("veps4", [P, TPC])
        half_rstd = sb("half_rstd", [P, TPC])
        rstd = sb("rstd", [P, TPC])
        nmr = sb("nmr", [P, TPC])
        xln = sb("xln", [P, TPC, D])
        xln_t = sb("xln_t", [P, CHUNK])
        ctx_tr = [sb(f"ctx_tr{i}", [P, CHUNK]) for i in range(2)]
        parts = [sb(f"parts{i}", [P, 2, 2, CHUNK], F16) for i in range(2)]
        k_stack = [sb(f"k_stack{i}", [P, GROUPS, CHUNK], F16) for i in range(2)]
        q_stack = [sb(f"q_stack{i}", [P, GROUPS, SLOTS, CHUNK], F16) for i in range(2)]
        v_diag = [sb(f"v_diag{i}", [P, PPC * HEADS * 32]) for i in range(2)]
        negmax = [sb(f"negmax{i}", [P, SEQ], BF16) for i in range(2)]
        probs = [sb(f"probs{i}", [P, HEADS, SEQ]) for i in range(4)]
        zsum = [sb(f"zsum{i}", [P, SEQ]) for i in range(2)]
        rz = [sb(f"rz{i}", [P, SEQ]) for i in range(4)]
        att_t = [sb(f"att_t{i}", [P, 2, CHUNK // 2]) for i in range(2)]
        st2 = [sb(f"st2_{i}", [P, 2 * TPC, 6]) for i in range(2)]
        ag2 = [sb(f"ag2_{i}", [P, 4, 2 * TPC]) for i in range(2)]
        ve2 = [sb(f"ve2_{i}", [P, 2 * TPC]) for i in range(2)]
        nm2 = [sb(f"nm2_{i}", [P, 2 * TPC]) for i in range(2)]
        rs2 = [sb(f"rs2_{i}", [P, 2 * TPC]) for i in range(2)]
        nmr2 = [sb(f"nmr2_{i}", [P, 2 * TPC]) for i in range(2)]
        z = [[sb(f"z{v}_{i}", [P, TPC, D]) for i in range(2 if v == 0 else 1)] for v in range(4)]
        h = [[sb(f"h{v}_{i}", [P, CHUNK]) for i in range(2 if v < 3 else 1)] for v in range(4)]
        g = [sb(f"g{i}", [P, CHUNK]) for i in range(3)]

        score_ps = [ps(f"score_ps{i}", [P, HEADS * SEQ]) for i in range(2)]
        att_ps = ps("att_ps", [P, CHUNK])
        wo_ps = ps("wo_ps", [P, CHUNK])
        work0 = ps("work0", [P, CHUNK])
        work1 = ps("work1", [P, CHUNK])
        bank = [score_ps[0][:, 0:CHUNK], score_ps[0][:, CHUNK:], score_ps[1][:, 0:CHUNK], score_ps[1][:, CHUNK:],
                att_ps[:, :], wo_ps[:, :], work0[:, :], work1[:, :]]

        s_qk_load = sem("s_qk_load")
        s_row_load = sem("s_row_load")
        s_vo_load = sem("s_vo_load")
        s_fload = sem("s_fload")
        s_const = sem("s_const")
        s_cast = sem("s_cast")
        s_wperm = sem("s_wperm")
        s_split = sem("s_split")
        s_tr = sem("s_tr")
        s_wready = sem("s_wready")
        s_pick = sem("s_pick")
        s_deq = sem("s_deq")
        s_lbt_ps = sem("s_lbt_ps")
        s_lbt = sem("s_lbt")
        s_lora = sem("s_lora")
        s_weff = sem("s_weff")
        s_lint_ps = sem("s_lint_ps")
        s_lint = sem("s_lint")
        s_xin = [sem(f"s_xin{i}") for i in range(3)]
        s_xnext = [sem(f"s_xnext{i}") for i in range(2)]
        s_ctxin = [sem(f"s_ctxin{i}") for i in range(2)]
        s_aggr = sem("s_aggr")
        s_bn = sem("s_bn")
        s_rstd = sem("s_rstd")
        s_nmr = sem("s_nmr")
        s_xln = sem("s_xln")
        s_xln_ps = sem("s_xln_ps")
        s_xln_t = sem("s_xln_t")
        s_ctx_ps = sem("s_ctx_ps")
        s_ctx_t = sem("s_ctx_t")
        s_q_ps, s_k_ps = sem("s_q_ps"), sem("s_k_ps")
        s_q_hi, s_k_hi = sem("s_q_hi"), sem("s_k_hi")
        s_q_rest, s_k_rest = sem("s_q_rest"), sem("s_k_rest")
        s_q_lo, s_k_lo = sem("s_q_lo"), sem("s_k_lo")
        s_q_out, s_k_out = sem("s_q_out"), sem("s_k_out")
        s_stack = [sem(f"s_stack{i}") for i in range(2)]
        s_v_ps = sem("s_v_ps")
        s_v = sem("s_v")
        s_att_t = sem("s_att_t")
        s_wo = sem("s_wo")
        s_x2 = sem("s_x2")
        s_scores = sem("s_scores")
        s_negmax = sem("s_negmax")
        s_shifted = sem("s_shifted")
        s_exp = sem("s_exp")
        s_zsum = sem("s_zsum")
        s_rz = sem("s_rz")
        s_probs = sem("s_probs")
        s_pv = sem("s_pv")
        p_bn = [sem(f"p_bn{b}") for b in range(2)]
        p_mv = [sem(f"p_mv{b}") for b in range(2)]
        p_st = [sem(f"p_st{b}") for b in range(2)]
        p_rs = [sem(f"p_rs{b}") for b in range(2)]
        p_nmr = [sem(f"p_nmr{b}") for b in range(2)]
        p_z0 = sem("p_z0_scaled")
        p_y = [sem(f"p_y{v}") for v in range(4)]
        p_z = [sem(f"p_z{v}") for v in range(4)]
        p_zt = [sem(f"p_zt{v}") for v in range(4)]
        p_g = [sem(f"p_g{v}") for v in range(4)]
        p_c = [sem(f"p_c{v}") for v in range(4)]
        p_h = [sem(f"p_h{v}") for v in range(4)]
        p_ht = sem("p_ht")
        p_out = sem("p_out")
        s_store = sem("s_store")

        def live(c):
            return not isinstance(c, int) or 0 <= c < NCHUNK

        def some(count):
            return not isinstance(count, int) or count > 0

        def query0(pair, b):
            return 256 * (pair // 2) + SEQ * (pair % 2) + TILE * b

        def early_steps(c, p, step):
            if isinstance(c, int):
                for t, place in EARLY.items():
                    if place == (c, p):
                        step(t, t % 2)

        def chunks(eng, body):
            for c in range(-3, 2):
                body(c, c % 2, c // 2)
            with eng.Fori(1, 6) as i:
                body(2 * i, 0, i)
                body(2 * i + 1, 1, i)
            for c in range(12, NCHUNK + 2):
                body(c, c % 2, c // 2)

        def steps(eng, body):
            for t in range(FIRST_STEP, 8):
                body(t, t % 2)
            with eng.Fori(4, 7) as i:
                body(2 * i, 0)
                body(2 * i + 1, 1)
            for t in range(14, NCHUNK + STAGES - 1):
                body(t, t % 2)

        def product_bank(i):
            return bank[i % 4][:, P * (i // 4):P * (i // 4 + 1)]

        def layer_bank(i):
            return bank[(4, 5, 3)[i // 2]][:, P * (i % 2):P * (i % 2 + 1)]

        def first_layer_bank(v, t, par):
            if v == 1 and isinstance(t, int) and t < FIRST_STEP:
                return bank[6 if t == 2 else 2]
            return bank[(5 if par else 2) if v == 1 else 3 - v]

        def last_bank(par):
            return bank[2 if par else 5]

        def transpose_bank(v, t, par):
            if isinstance(t, int) and t < FIRST_STEP:
                return bank[3]
            return (None, last_bank(par), bank[4], bank[3])[v]

        def second_layer_bank(v, t):
            return bank[6] if isinstance(t, int) and t < FIRST_STEP else (None, bank[4], bank[3], bank[6])[v]

        block = es.enter_context(nc.Block())

        @block.sync
        def _(sp):
            sp.dma_start(x_all[:, 0, :, :], x_t[0]).then_inc(s_xin[0], 16)
            for k, src in (("q", wq), ("k", wk)):
                sp.dma_start(w_in[k][:, :], src).then_inc(s_qk_load, 16)
            sp.dma_start(ctx_sb[0][:, :, :], ctx_t[0]).then_inc(s_ctxin[0], 16)
            for r, src in ((ROW_BQ, bq), (ROW_BK, bk), (ROW_BV, bv), (ROW_BO, bo)):
                sp.dma_start(rows[r:r + 1, :], src.rearrange("(a n) -> a n", a=1)).then_inc(s_row_load, 16)
            sp.dma_start(rows[ROW_BL:ROW_BL + NLIN, :], qb).then_inc(s_row_load, 16)
            sp.dma_start(rows[ROW_GAMMA:ROW_GAMMA + NBLK, :], gamma).then_inc(s_row_load, 16)
            sp.dma_start(rows[ROW_BETA:ROW_BETA + NBLK, :], beta).then_inc(s_row_load, 16)
            sp.dma_start(x_all[:, 1, :, :], x_t[1]).then_inc(s_xin[1], 16)
            for k, src in (("v", wv), ("o", wo)):
                sp.dma_start(w_in[k][:, :], src).then_inc(s_vo_load, 16)

            def chunk(c, par, half):
                if isinstance(c, int) and c == -2:
                    sp.dma_start(x_all[:, 2:4, :, :], x_pt[:, 2:4, :, :]).then_inc(s_xin[2], 16)
                    sp.dma_start(qw_in[:, :, :], qw.rearrange("l o d -> o l d")).then_inc(s_fload, 16)
                    sp.dma_start(qs_in[:, :, :], qs.rearrange("l o s -> o l s")).then_inc(s_fload, 16)
                    la_rows = la.rearrange("l r d -> (l r) d")
                    sp.dma_start(la_in[0][:, :], la_rows[0:P, :]).then_inc(s_fload, 16)
                    sp.dma_start(la_in[1][:, :], la_rows[P:, :]).then_inc(s_fload, 16)
                    sp.dma_start(lb_in[:, :, :], lb.rearrange("l o r -> o l r")).then_inc(s_fload, 16)
                if live(c + 2):
                    sp.wait_ge(s_q_lo, c + 3)
                    sp.dma_start(q_dram[c + 2], parts[par][:, 0, :, :].rearrange("f l t -> f (l t)").unsqueeze(1)
                                 .broadcast_to([P, 2, 2 * CHUNK])).then_inc(s_q_out, 16)
                if live(c + 4):
                    if live(c + 2):
                        sp.wait_ge(s_ctx_ps, c + 3)
                    sp.dma_start(ctx_sb[par][:, :, :], ctx_t[c + 4]).then_inc(s_ctxin[par], 16)
                    if not isinstance(c, int) or c >= 0:
                        sp.dma_start(x_all[:, c + 4, :, :], x_t[c + 4]).then_inc(s_xnext[par], 16)
                if live(c + 2):
                    if live(c):
                        sp.wait_ge(s_scores, PPC * (c + 1))
                    sp.wait_ge(s_k_lo, c + 3)
                    sp.dma_start(k_dram[c + 2], parts[par][:, 1, :, :]).then_inc(s_k_out, 16)
                    if isinstance(c, int) and c < 0:
                        sp.wait_ge(s_const, c + 8)
                    sp.wait_ge(s_q_out, 16 * (c + 3))
                    src = q_dram[c + 2].rearrange("(g s j) a (l t) -> s (j a l) g t", g=GROUPS, s=SLOTS, l=2)
                    for s in range(SLOTS):
                        r = ROWS_PER_SLOT * s
                        sp.dma_start(q_stack[par][r:r + ROWS_PER_SLOT, :, s, :], src[s]).then_inc(s_stack[par], 16)
                    sp.wait_ge(s_k_out, 16 * (c + 3))
                    src = k_dram[c + 2].rearrange("(g r) l t -> (r l) g t", g=GROUPS)
                    for a in range(2):
                        sp.dma_start(k_stack[par][a:P:2, :, :], src).then_inc(s_stack[par], 16)

            def step(t, par):
                k = t - 7
                if live(k):
                    sp.wait_ge(p_out, k + 1)
                    sp.dma_start(out_t[k], x_all[:, k, :, :]).then_inc(s_store, 16)

            chunks(sp, chunk)
            steps(sp, step)
            sp.wait_ge(s_store, 16 * NCHUNK)

        @block.gpsimd
        def _(pool):
            nc.gpsimd.memset(ident[:, :], 0.0).then_inc(s_const, 1)
            pool.wait_ge(s_const, 1)
            nc.gpsimd.affine_select(out=ident[:, :], in_=ident[:, :], compare_op=ALU.not_equal, fill=1.0, base=0,
                                    pattern=[[-1, P]], channel_multiplier=1).then_inc(s_const, 1)
            nc.gpsimd.memset(minus_half[:, :], -0.5).then_inc(s_const, 1)
            pool.wait_ge(s_const, 3)
            def chunk(c, par, half):
                if isinstance(c, int) and c == -2:
                    nc.gpsimd.memset(bias3[:, :], 0.0).then_inc(s_const, 1)
                    nc.gpsimd.memset(wo_split[:, :, :, :], 0.0).then_inc(s_const, 1)
                    nc.gpsimd.memset(q_stack[0][:, :, :, :].bitcast(F32), 0.0).then_inc(s_const, 1)
                if isinstance(c, int) and c == -1:
                    nc.gpsimd.memset(q_stack[1][:, :, :, :].bitcast(F32), 0.0).then_inc(s_const, 1)
                for p in range(PPC):
                    n = PPC * c + p
                    mc = c - (p == 0)
                    if live(mc):
                        m = n - 1
                        pool.wait_ge(s_rz, m + 1)
                        e = probs[(p - 1) % 4]
                        nc.gpsimd.tensor_tensor(e[:, :, :], e[:, :, :],
                                                rz[(p - 1) % 4][:, :].unsqueeze(1).broadcast_to([P, HEADS, SEQ]),
                                                ALU.mult).then_inc(s_probs, 1)
                    if p == 1 and live(c + 3):
                        pool.wait_ge(s_bn, c + 4)
                        if some(c + 3):
                            pool.wait_ge(s_xln, c + 3)
                        nc.gpsimd.tensor_tensor(agg[:, 0, :], stats[:, :, 1], stats[:, :, 4], ALU.add)
                        nc.gpsimd.tensor_tensor(agg[:, 1, :], stats[:, :, 2], stats[:, :, 5], ALU.add)
                        nc.gpsimd.tensor_tensor(agg[:, 2, :], stats[:, :, 1], stats[:, :, 4],
                                                ALU.subtract).then_inc(s_aggr, 1)
                        pool.wait_ge(s_aggr, 3 * (c + 3) + 1)
                        nc.gpsimd.tensor_tensor(agg[:, 3, :], agg[:, 2, :], agg[:, 2, :], ALU.mult)
                        nc.gpsimd.tensor_scalar(neg2mean[:, :], agg[:, 0, :], -1.0, None, ALU.mult)
                        nc.gpsimd.tensor_scalar(agg[:, 1, :], agg[:, 1, :], 4.0 / D, 4.0 * EPS, ALU.mult,
                                                ALU.add).then_inc(s_aggr, 1)
                        pool.wait_ge(s_aggr, 3 * (c + 3) + 2)
                        nc.gpsimd.tensor_tensor(veps4[:, :], agg[:, 1, :], agg[:, 3, :], ALU.add).then_inc(s_aggr, 1)
                        pool.wait_ge(s_aggr, 3 * (c + 3) + 3)
                        nc.gpsimd.tensor_tensor(half_rstd[:, :], veps4[:, :], minus_half[:, 0:TPC],
                                                ALU.pow).then_inc(s_rstd, 1)
                        pool.wait_ge(s_rstd, c + 4)
                        nc.gpsimd.tensor_tensor(nmr[:, :], neg2mean[:, :], half_rstd[:, :], ALU.mult)
                        nc.gpsimd.tensor_scalar(rstd[:, :], half_rstd[:, :], 2.0, None, ALU.mult).then_inc(s_nmr, 1)
                    if isinstance(c, int) and c == -1 and p == 1:
                        for i in range(2):
                            nc.gpsimd.memset(v_diag[i][:, :], 0.0).then_inc(s_const, 1)
                    early_steps(c, p, step)


            def norm_scales(b, lo, hi, count):
                pool.wait_ge(p_st[b], count)
                nc.gpsimd.tensor_tensor(rs2[b][:, lo:hi], ve2[b][:, lo:hi], minus_half[:, lo:hi],
                                        ALU.pow).then_inc(p_rs[b], 1)
                pool.wait_ge(p_rs[b], count)
                nc.gpsimd.tensor_tensor(nmr2[b][:, lo:hi], nm2[b][:, lo:hi], rs2[b][:, lo:hi],
                                        ALU.mult).then_inc(p_nmr[b], 1)

            def step(t, par):
                if live(t) or live(t - 6):
                    if live(t - 7):
                        pool.wait_ge(p_z[3], t - 6)
                    norm_scales(0, 0 if live(t) else TPC, 2 * TPC if live(t - 6) else TPC, t + 1)
                if live(t - 4) or live(t - 2):
                    if live(t - 5):
                        pool.wait_ge(p_z[2], t - 4)
                    if live(t - 3):
                        pool.wait_ge(p_z[1], t - 2)
                    norm_scales(1, 0 if live(t - 4) else TPC, 2 * TPC if live(t - 2) else TPC, t - 1)
                if live(t):
                    if some(t - 1):
                        pool.wait_ge(p_zt[0], t - 1)
                    nc.gpsimd.tensor_tensor(z[0][par][:, :, :], x_all[:, t, :, :],
                                            rs2[0][:, 0:TPC].unsqueeze(2).broadcast_to([P, TPC, D]),
                                            ALU.mult).then_inc(p_z0, 1)
                    pool.wait_ge(p_nmr[0], t + 1)
                    pool.wait_ge(p_z0, t + 1)
                    nc.gpsimd.tensor_tensor(z[0][par][:, :, :], z[0][par][:, :, :],
                                            nmr2[0][:, 0:TPC].unsqueeze(2).broadcast_to([P, TPC, D]),
                                            ALU.add).then_inc(p_z[0], 1)

            chunks(pool, chunk)
            steps(pool, step)

        @block.vector
        def _(dve):
            dve.wait_ge(s_const, 2)
            nc.vector.tensor_copy(ident_bf[:, :], ident[:, :]).then_inc(s_cast, 1)
            nc.vector.tensor_scalar(neg_ident[:, :], ident[:, :], -1.0, None, ALU.mult).then_inc(s_cast, 1)
            def small_weights():
                nc.vector.tensor_tensor(pick_a[:, :], ident[:, 0:NROWS], ident[:, 32:32 + NROWS], ALU.add).then_inc(s_pick, 1)
                dve.wait_ge(s_pick, 1)
                nc.vector.tensor_tensor(pick[:, :], pick_a[:, :], ident[:, 64:64 + NROWS], ALU.add).then_inc(s_pick, 1)
                dve.wait_ge(s_pick, 2)
                for i, r in enumerate(BIAS_ROWS):
                    nc.vector.tensor_copy(pick_row[:, i, :], pick[:, r:r + 1].broadcast_to([P, P])).then_inc(s_pick, 1)
                dve.wait_ge(s_row_load, 16 * 7)
                nc.vector.tensor_copy(rows_h[:, :].rearrange("p (h j) -> p h j", j=DH),
                                      rows[:, :].rearrange("p (j h) -> p h j", j=DH)).then_inc(s_wperm, 1)
                dve.wait_ge(s_const, 5)
                nc.vector.tensor_copy(bias3[0:NROWS, :], rows[:, :]).then_inc(s_split, 1)
                dve.wait_ge(s_split, 1)
                nc.vector.tensor_tensor(row_r1[:, :], rows[:, :], bias3[0:NROWS, :], ALU.subtract).then_inc(s_split, 1)
                dve.wait_ge(s_split, 2)
                nc.vector.tensor_copy(bias3[32:32 + NROWS, :], row_r1[:, :]).then_inc(s_split, 1)
                nc.vector.tensor_copy(row_mid[:, :], row_r1[:, :]).then_inc(s_split, 1)
                dve.wait_ge(s_split, 4)
                nc.vector.tensor_tensor(row_r2[:, :], row_r1[:, :], row_mid[:, :],
                                        ALU.subtract).then_inc(s_split, 1)
                dve.wait_ge(s_split, 5)
                nc.vector.tensor_copy(bias3[64:64 + NROWS, :], row_r2[:, :]).then_inc(s_split, 1)
                dve.wait_ge(s_vo_load, 16 * 2)
                wo_cols = w_in["o"][:, :].rearrange("p (j o u) -> p o u j", o=2, u=8)
                for o in range(2):
                    for b in range(2):
                        dst = wo_split[:, o, b, :].rearrange("p (u b j) -> p b u j", u=8, b=2)
                        nc.vector.tensor_copy(dst[:, b], wo_cols[:, o]).then_inc(s_wperm, 1)

            def feed_forward_weights():
                dve.wait_ge(s_fload, 16 * 5)
                nc.vector.tensor_scalar(w_deq[:, :, :], qw_in[:, :, :], 1.0 / 7.5, -1.0, ALU.mult,
                                        ALU.add).then_inc(s_deq, 1)
                dve.wait_ge(s_deq, 1)
                nc.vector.tensor_tensor(
                    w_deq[:, :, :].rearrange("p l (s e) -> p (l s) e", e=GROUP),
                    w_deq[:, :, :].rearrange("p l (s e) -> p (l s) e", e=GROUP),
                    qs_in[:, :, :].rearrange("p l s -> p (l s)").unsqueeze(2).broadcast_to([P, NLIN * NSC, GROUP]),
                    ALU.mult).then_inc(s_deq, 1)
                dve.wait_ge(s_lbt_ps, 2)
                nc.vector.tensor_copy(lb_t[0][:, :], bank[0][:, 0:P]).then_inc(s_lbt, 1)
                nc.vector.tensor_copy(lb_t[1][:, :], bank[1][0:2 * RANK, 0:P]).then_inc(s_lbt, 1)
                dve.wait_ge(s_deq, 2)
                dve.wait_ge(s_lora, NLIN)
                for i in range(NLIN):
                    nc.vector.tensor_tensor(w_eff[:, i, :], product_bank(i), w_deq[:, i, :],
                                            ALU.add).then_inc(s_weff, 1)

            def combine(k, bn_done, step_done, used, done, st, ag, ve, nm):
                dve.wait_ge(bn_done, k + 1)
                nc.vector.tensor_tensor(ag[:, 0, :], st[:, :, 1], st[:, :, 4], ALU.add)
                nc.vector.scalar_tensor_tensor(ag[:, 1, :], st[:, :, 2], EPS * D, st[:, :, 5], ALU.add, ALU.add)
                nc.vector.tensor_tensor(ag[:, 2, :], st[:, :, 1], st[:, :, 4], ALU.subtract).then_inc(step_done, 1)
                dve.wait_ge(step_done, 2 * k + 1)
                if some(k):
                    dve.wait_ge(used, k)
                nc.vector.scalar_tensor_tensor(ag[:, 3, :], ag[:, 2, :], 0.25, ag[:, 2, :], ALU.mult, ALU.mult)
                nc.vector.tensor_scalar(nm[:, :], ag[:, 0, :], -0.5, None, ALU.mult).then_inc(step_done, 1)
                dve.wait_ge(step_done, 2 * k + 2)
                nc.vector.scalar_tensor_tensor(ve[:, :], ag[:, 1, :], 1.0 / D, ag[:, 3, :], ALU.mult,
                                               ALU.add).then_inc(done, 1)

            def chunk(c, par, half):
                if isinstance(c, int) and c == -2:
                    small_weights()
                for p in range(PPC):
                    n = PPC * c + p
                    if live(c):
                        dve.wait_ge(s_scores, n + 1)
                        if some(n - 1):
                            dve.wait_ge(s_shifted, n - 1)
                        nc.vector.tensor_reduce(negmax[p % 2][:, :],
                                                score_ps[p % 2][:, :].rearrange("p (h k) -> p k h", k=SEQ),
                                                AX_X, ALU.max, negate=True).then_inc(s_negmax, 1)
                    if p == 1 and live(c + 3):
                        if isinstance(c, int) and c + 3 < 3:
                            dve.wait_ge(s_xin[c + 3], 16)
                        elif not isinstance(c, int) or c + 3 >= 4:
                            dve.wait_ge(s_xnext[1 - par], 16 * (half + par))
                        if some(c + 3):
                            dve.wait_ge(s_rstd, c + 3)
                        for t in range(TPC):
                            ins = nc.vector.bn_stats(stats[:, t, :], x_all[:, c + 3, t, :])
                        ins.then_inc(s_bn, 1)
                    if isinstance(c, int) and c == -1 and p == 1:
                        feed_forward_weights()
                    mc = c - (p == 0)
                    if live(mc):
                        m = n - 1
                        q = (p - 1) % 2
                        dve.wait_ge(s_exp, m + 1)
                        nc.vector.tensor_reduce(zsum[q][:, :], probs[(p - 1) % 4][:, :, :].rearrange("p h k -> p k h"),
                                                AX_X, ALU.add).then_inc(s_zsum, 1)
                        dve.wait_ge(s_zsum, m + 1)
                        nc.vector.reciprocal(rz[(p - 1) % 4][:, :], zsum[q][:, :]).then_inc(s_rz, 1)
                    if p == 3 and live(c - 2):
                        dve.wait_ge(s_wo, c - 1)
                        nc.vector.tensor_tensor(x_all[:, c - 2, :, :],
                                                wo_ps[:, :].rearrange("p (t d) -> p t d", t=TPC),
                                                x_all[:, c - 2, :, :], ALU.add).then_inc(s_x2, 1)
                    early_steps(c, p, step)



            def batch_stats(b, lo, hi, count):
                combine(count - 1, p_bn[b], p_mv[b], p_nmr[b], p_st[b], st2[b][:, lo:hi, :], ag2[b][:, :, lo:hi],
                        ve2[b][:, lo:hi], nm2[b][:, lo:hi])

            def input_stats(k):
                for i in range(TPC):
                    ins = nc.vector.bn_stats(st2[0][:, i, :], x_all[:, k, i, :])
                if isinstance(k, int) and k <= FIRST_STEP:
                    ins.then_inc(p_bn[0], 1)

            def step(t, par):
                if isinstance(t, int) and t <= FIRST_STEP:
                    dve.wait_ge(s_x2, t + 1 if t < FIRST_STEP else NCHUNK)
                if live(t) and isinstance(t, int) and t <= FIRST_STEP:
                    input_stats(t)
                if live(t - 6):
                    dve.wait_ge(p_y[3], t - 5)
                    for i in range(TPC):
                        ins = nc.vector.bn_stats(st2[0][:, TPC + i, :], bank[0][:, TILE * i:TILE * (i + 1)])
                    ins.then_inc(p_bn[0], 1)
                if live(t) or live(t - 6):
                    batch_stats(0, 0 if live(t) else TPC, 2 * TPC if live(t - 6) else TPC, t + 1)
                if live(t - 4):
                    dve.wait_ge(p_y[2], t - 3)
                    for i in range(TPC):
                        ins = nc.vector.bn_stats(st2[1][:, i, :], bank[1][:, TILE * i:TILE * (i + 1)])
                if live(t - 2):
                    dve.wait_ge(p_y[1], t - 1)
                    for i in range(TPC):
                        ins = nc.vector.bn_stats(st2[1][:, TPC + i, :], first_layer_bank(1, t, par)[:, TILE * i:TILE * (i + 1)])
                if live(t - 4) or live(t - 2):
                    ins.then_inc(p_bn[1], 1)
                    batch_stats(1, 0 if live(t - 4) else TPC, 2 * TPC if live(t - 2) else TPC, t - 1)
                if not isinstance(t, int) or (t >= FIRST_STEP and live(t + 1)):
                    input_stats(t + 1)
                for v, k in ((3, t - 7), (2, t - 5), (1, t - 3)):
                    if live(k):
                        q = (par - 2 * v - 1) % 2
                        dve.wait_ge(p_c[v], k + 1)
                        if v == 3:
                            if some(k):
                                dve.wait_ge(p_ht, k)
                        elif some(k - 1):
                            dve.wait_ge(p_h[v + 1], k - 1)
                        nc.vector.scalar_tensor_tensor(h[v][0 if v == 3 else q][:, :], second_layer_bank(v, t),
                                                       cols[:, ROW_BL + 2 * v - 1:ROW_BL + 2 * v],
                                                       h[v - 1][q][:, :], ALU.add, ALU.add).then_inc(p_h[v], 1)
                if live(t - 7):
                    k = t - 7
                    dve.wait_ge(p_ht, k + 1)
                    nc.vector.tensor_tensor(x_all[:, k, :, :], last_bank(par).rearrange("p (t d) -> p t d", t=TPC),
                                            x_all[:, k, :, :], ALU.add).then_inc(p_out, 1)

            chunks(dve, chunk)
            steps(dve, step)

        @block.scalar
        def _(act):
            def transposed(i):
                act.wait_ge(s_tr, (1, 2, 4)[i])
                nc.scalar.activation(w_t["qkv"[i]][:, :].rearrange("p (h j) -> p h j", j=DH),
                                     bank[i][:, 0:P].rearrange("p (j h) -> p h j", j=DH), ACT.Copy).then_inc(s_wready, 1)

            transposed(0)
            transposed(1)

            def transposed_layers():
                for u in range(NLIN // 2):
                    act.wait_ge(s_lint_ps, u + 1)
                    for i in (2 * u, 2 * u + 1):
                        ins = nc.scalar.activation(lin_t[:, i, :], layer_bank(i), ACT.Copy)
                    ins.then_inc(s_lint, 2)

            def chunk(c, par, half):
                if isinstance(c, int) and c == -2:
                    act.wait_ge(s_tr, 3)
                    nc.scalar.activation(cols[:, :], bank[3][:, 0:NROWS], ACT.Copy).then_inc(s_wready, 1)
                    nc.scalar.activation(cols_h[:, :], bank[3][:, NROWS:2 * NROWS], ACT.Copy).then_inc(s_wready, 1)
                if isinstance(c, int) and c == -1:
                    transposed(2)
                    act.wait_ge(s_tr, 5)
                    nc.scalar.activation(wo_t[:, :, :, :].rearrange("p o b n -> p (o b n)"), bank[4],
                                         ACT.Copy).then_inc(s_wready, 1)

                def exponentials(p):
                    n = PPC * c + p
                    act.wait_ge(s_shifted, n + 1)
                    if some(n - 3):
                        act.wait_ge(s_pv, n - 3)
                    nc.scalar.activation(probs[p][:, :, :].rearrange("p h k -> p (h k)"), score_ps[p % 2][:, :],
                                         ACT.Exp, scale=SCALE).then_inc(s_exp, 1)

                def normalised_input(k):
                    if live(k):
                        act.wait_ge(s_nmr, k + 1)
                        if some(k):
                            act.wait_ge(s_xln_ps, k)
                        for t in range(TPC):
                            ins = nc.scalar.activation(xln[:, t, :], x_all[:, k, t, :], ACT.Identity,
                                                       bias=nmr[:, t:t + 1], scale=rstd[:, t:t + 1])
                        ins.then_inc(s_xln, 1)

                if live(c):
                    exponentials(0)
                if live(c + 2):
                    act.wait_ge(s_ctx_ps, c + 3)
                    if some(c + 1):
                        act.wait_ge(s_v_ps, c + 1)
                    nc.scalar.activation(ctx_tr[par][:, :], work1[:, :], ACT.Copy).then_inc(s_ctx_t, 1)
                    act.wait_ge(s_xln_ps, c + 3)
                    if some(c + 2):
                        act.wait_ge(s_q_ps, c + 2)
                    nc.scalar.activation(xln_t[:, :], work0[:, :], ACT.Copy).then_inc(s_xln_t, 1)
                if isinstance(c, int) and c == -1:
                    normalised_input(c + 3)
                early_steps(c, 0, step)
                if live(c):
                    exponentials(1)
                if live(c + 2):
                    act.wait_ge(s_q_ps, c + 3)
                    if some(c + 1):
                        act.wait_ge(s_q_out, 16 * (c + 1))
                    if isinstance(c, int) and c == -2:
                        act.wait_ge(s_wready, 4)
                    nc.scalar.activation(parts[par][:, 0, 0, :], work0[:, :], ACT.Identity,
                                         bias=cols_h[:, ROW_BQ:ROW_BQ + 1]).then_inc(s_q_hi, 1)
                    act.wait_ge(s_q_rest, c + 3)
                    nc.scalar.activation(parts[par][:, 0, 1, :], work0[:, :], ACT.Identity,
                                         bias=cols_h[:, ROW_BQ:ROW_BQ + 1]).then_inc(s_q_lo, 1)
                early_steps(c, 1, step)
                if live(c - 1):
                    act.wait_ge(s_pv, PPC * c)
                    if some(c - 2):
                        act.wait_ge(s_wo, c - 2)
                    nc.scalar.activation(att_t[1 - par][:, :, :].rearrange("p o t -> p (o t)"), att_ps[:, :],
                                         ACT.Copy).then_inc(s_att_t, 1)
                if live(c):
                    exponentials(2)
                if live(c + 2):
                    act.wait_ge(s_k_ps, c + 3)
                    if some(c + 1):
                        act.wait_ge(s_k_out, 16 * (c + 1))
                    nc.scalar.activation(parts[par][:, 1, 0, :], work1[:, :], ACT.Identity,
                                         bias=cols_h[:, ROW_BK:ROW_BK + 1]).then_inc(s_k_hi, 1)
                    act.wait_ge(s_k_rest, c + 3)
                    nc.scalar.activation(parts[par][:, 1, 1, :], work1[:, :], ACT.Identity,
                                         bias=cols_h[:, ROW_BK:ROW_BK + 1]).then_inc(s_k_lo, 1)
                if isinstance(c, int) and c == -1:
                    transposed_layers()
                early_steps(c, 2, step)
                if live(c):
                    exponentials(3)
                if not isinstance(c, int) or c != -1:
                    normalised_input(c + 3)
                if live(c + 1):
                    act.wait_ge(s_v_ps, c + 2)
                    if live(c - 1):
                        act.wait_ge(s_pv, PPC * c)
                    elif isinstance(c, int) and c == -1:
                        act.wait_ge(s_const, 9)
                    for b in range(2):
                        dst = v_diag[1 - par][SEQ * b:SEQ * (b + 1), :].rearrange("p (u a e) -> p u a e", a=4, e=16)
                        ins = nc.scalar.activation(
                            dst[:, :, 0:4:3, DH * b:DH * (b + 1)],
                            work0[SEQ * b:SEQ * (b + 1), :].rearrange("p (u s j) -> p u s j", s=2, j=DH), ACT.Copy)
                    ins.then_inc(s_v, 1)
                early_steps(c, 3, step)



            def normalise(v, k, b, lo, count, src):
                act.wait_ge(p_nmr[b], count)
                if some(k):
                    act.wait_ge(p_zt[v], k)
                for t in range(TPC):
                    ins = nc.scalar.activation(z[v][0][:, t, :], src[:, TILE * t:TILE * (t + 1)], ACT.Identity,
                                               bias=nmr2[b][:, lo + t:lo + t + 1], scale=rs2[b][:, lo + t:lo + t + 1])
                ins.then_inc(p_z[v], 1)

            def step(t, par):
                for v, k in ((3, t - 7), (2, t - 5), (1, t - 3)):
                    if live(k):
                        act.wait_ge(p_zt[v], k + 1)
                        if some(k):
                            act.wait_ge(p_c[v], k)
                        nc.scalar.activation(g[v - 1][:, :], transpose_bank(v, t, par), ACT.Gelu,
                                             bias=cols[:, ROW_BETA + v - 1:ROW_BETA + v],
                                             scale=cols[:, ROW_GAMMA + v - 1:ROW_GAMMA + v]).then_inc(p_g[v], 1)
                if live(t - 6):
                    normalise(3, t - 6, 0, TPC, t + 1, bank[0])
                if live(t - 4):
                    normalise(2, t - 4, 1, 0, t - 1, bank[1])
                if live(t - 1):
                    k = t - 1
                    act.wait_ge(p_zt[0], k + 1)
                    if some(k - 1):
                        act.wait_ge(p_h[1], k - 1)
                    nc.scalar.activation(h[0][(par - 1) % 2][:, :], bank[7], ACT.Copy).then_inc(p_h[0], 1)
                if live(t - 2):
                    normalise(1, t - 2, 1, TPC, t - 1, first_layer_bank(1, t, par))

            chunks(act, chunk)
            steps(act, step)

        @block.tensor
        def _(pe):
            pe.wait_ge(s_const, 2)
            pe.wait_ge(s_qk_load, 16 * 2)
            for i, k in enumerate("qk"):
                nc.tensor.transpose(bank[i][:, 0:P], w_in[k][:, :], ident[:, :]).then_inc(s_tr, 1)
            pe.wait_ge(s_wperm, 1)
            nc.tensor.transpose(bank[3][:, 0:NROWS], rows[:, :], ident[0:NROWS, 0:NROWS])
            nc.tensor.transpose(bank[3][:, NROWS:2 * NROWS], rows_h[:, :],
                                ident[0:NROWS, 0:NROWS]).then_inc(s_tr, 1)
            pe.wait_ge(s_wready, 2)
            pe.wait_ge(s_cast, 2)

            def value_and_output_weights():
                pe.wait_ge(s_vo_load, 16 * 2)
                nc.tensor.transpose(bank[2][:, 0:P], w_in["v"][:, :], ident[:, :]).then_inc(s_tr, 1)
                pe.wait_ge(s_wperm, 5)
                for o in range(2):
                    for b in range(2):
                        ins = nc.tensor.transpose(bank[4][:, P * (2 * o + b):P * (2 * o + b + 1)],
                                                  wo_split[:, o, b, :], ident[:, :])
                ins.then_inc(s_tr, 1)

            def low_rank_columns():
                pe.wait_ge(s_fload, 16 * 5)
                lb_cols = lb_in[:, :, :].rearrange("p l r -> p (l r)")
                nc.tensor.transpose(bank[0][:, 0:P], lb_cols[:, 0:P], ident[:, :]).then_inc(s_lbt_ps, 1)
                nc.tensor.transpose(bank[1][0:2 * RANK, 0:P], lb_cols[:, P:], ident[:, :]).then_inc(s_lbt_ps, 1)

            def low_rank_products():
                pe.wait_ge(s_lbt, 2)
                pe.wait_ge(s_wready, 5)
                for i in range(NLIN):
                    r = RANK * (i % 4)
                    nc.tensor.matmul(product_bank(i), lb_t[i // 4][r:r + RANK, :], la_in[i // 4][r:r + RANK, :],
                                     start=True, stop=True).then_inc(s_lora, 1)

            def transpose_layers(u):
                pe.wait_ge(s_weff, 2 * u + 2)
                for i in (2 * u, 2 * u + 1):
                    ins = nc.tensor.transpose(layer_bank(i), w_eff[:, i, :], ident[:, :])
                ins.then_inc(s_lint_ps, 1)

            def bias_rows(dst, which, head_major=False):
                src = bias3[:, :].rearrange("p (j h) -> p h j", j=DH) if head_major else bias3[:, :]
                src = src.unsqueeze(1).broadcast_to([P, TPC] + list(src.shape[1:]))
                nc.tensor.matmul(dst, pick_row[:, which, :], src, start=True, stop=False, skip_group_check=True)

            def project_out(t, att):
                b, u = t % 2, t // 2
                for o in range(2):
                    ins = nc.tensor.matmul(wo_ps[:, TILE * t:TILE * (t + 1)], att[:, o, TILE * u:TILE * (u + 1)],
                                           wo_t[:, o, b, :], start=False, stop=o == 1, skip_group_check=True)
                return ins

            def chunk(c, par, half):
                if isinstance(c, int) and c == -1:
                    value_and_output_weights()
                    low_rank_columns()
                for p in range(PPC):
                    n = PPC * c + p
                    if isinstance(c, int) and c == -1:
                        if p == 1:
                            low_rank_products()
                        elif p == 3:
                            transpose_layers(2)
                            pe.wait_ge(s_pick, 2 + len(BIAS_ROWS))
                            pe.wait_ge(s_split, 6)
                    mc, mp = (c, p + 1) if p < 3 else (c + 1, 0)
                    if live(mc):
                        m = n + 1
                        mpar = mp % 2
                        mb = par if p < 3 else 1 - par
                        if mp == 0:
                            mh = half if par == 0 else half + 1
                            pe.wait_ge(s_stack[mb], 16 * STACK_DMAS * (mh + 1))
                        if some(m - 1):
                            pe.wait_ge(s_exp, m - 1)
                        elif isinstance(m, int) and m == 1:
                            pe.wait_ge(s_lint, NLIN)
                        for grp in range(GROUPS):
                            for b in range(2):
                                q0, k0 = query0(mp, b), TILE * mp + SEQ * b
                                ins = nc.tensor.matmul(
                                    score_ps[mpar][SEQ * b:SEQ * (b + 1), 256 * grp:256 * (grp + 1)],
                                    k_stack[mb][:, grp, k0:k0 + SEQ], q_stack[mb][:, grp, :, q0:q0 + SEQ],
                                    start=grp % 2 == 0, stop=False, skip_group_check=True)
                        ins.then_inc(s_scores, 1)
                    if live(c):
                        pe.wait_ge(s_negmax, n + 1)
                        for o in range(2):
                            ins = nc.tensor.matmul(score_ps[p % 2][:, CHUNK * o:CHUNK * (o + 1)], ident_bf[:, :],
                                                   negmax[p % 2][:, :].unsqueeze(1).broadcast_to([P, 8, SEQ]),
                                                   start=False, stop=True, skip_group_check=True)
                        ins.then_inc(s_shifted, 1)
                    if p == 0 and live(c + 2):
                        pe.wait_ge(s_ctxin[par], 16 * (half + 2))
                        if some(c + 2):
                            pe.wait_ge(s_k_lo, c + 2)
                        dst = work1[:, :].rearrange("p (u v b k) -> p u b v k", u=2, v=2, b=2)
                        for t in range(TPC):
                            ins = nc.tensor.transpose(dst[:, t // 2, t % 2], ctx_sb[par][:, t, :], ident[:, :])
                        ins.then_inc(s_ctx_ps, 1)
                    if p == 1 and live(c + 2):
                        pe.wait_ge(s_xln_t, c + 3)
                        nc.tensor.matmul(work0[:, :], w_t["q"][:, :], xln_t[:, :], start=True, stop=False,
                                         skip_group_check=True).then_inc(s_q_ps, 1)
                    if p == 2 and live(c + 2):
                        pe.wait_ge(s_ctx_t, c + 3)
                        nc.tensor.matmul(work1[:, :], w_t["k"][:, :], ctx_tr[par][:, :], start=True, stop=False,
                                         skip_group_check=True).then_inc(s_k_ps, 1)
                    if p == 3 and live(c + 1):
                        if live(c + 2):
                            pe.wait_ge(s_q_lo, c + 3)
                        elif some(c + 1):
                            pe.wait_ge(s_v, c + 1)
                        bias_rows(work0[:, :], 0, head_major=True)
                        for q in range(PPC):
                            ins = nc.tensor.matmul(work0[:, TILE * q:TILE * (q + 1)],
                                                   ctx_tr[1 - par][:, TILE * q:TILE * (q + 1)], w_t["v"][:, :],
                                                   start=False, stop=True, skip_group_check=True)
                        ins.then_inc(s_v_ps, 1)
                    if p == 3 and live(c - 1):
                        pe.wait_ge(s_att_t, c)
                        if some(c - 1):
                            pe.wait_ge(s_x2, c - 1)
                        bias_rows(wo_ps[:, :], 1)
                        project_out(0, att_t[1 - par])
                    if p < 3 and live(c - 2):
                        ins = project_out(p + 1, att_t[par])
                        if p == 2:
                            ins.then_inc(s_wo, 1)
                    mc, mp = (c, p - 2) if p >= 2 else (c - 1, p + 2)
                    if live(mc):
                        m = n - 2
                        mb = par if p >= 2 else 1 - par
                        pe.wait_ge(s_probs, m + 1)
                        if mp == 0:
                            pe.wait_ge(s_v, mc + 1)
                            if some(mc):
                                pe.wait_ge(s_att_t, mc)
                        for o in range(2):
                            for s in range(2):
                                for grp in range(4):
                                    hd = 8 * o + 2 * grp + s
                                    v0 = 32 * (HEADS * mp + hd)
                                    c0 = 256 * o + SEQ * mp
                                    ins = nc.tensor.matmul(
                                        att_ps[32 * grp:32 * (grp + 1), c0:c0 + SEQ], v_diag[mb][:, v0:v0 + 32],
                                        probs[mp][:, hd, :], start=(mp == 0 and o == 0 and s == 0),
                                        stop=False, skip_group_check=True, tile_position=(0, 32 * grp))
                        ins.then_inc(s_pv, 1)
                    if p == 0 and live(c + 2):
                        pe.wait_ge(s_xln, c + 3)
                        if some(c + 1):
                            pe.wait_ge(s_v, c + 1)
                        for t in range(TPC):
                            ins = nc.tensor.transpose(work0[:, TILE * t:TILE * (t + 1)], xln[:, t, :], ident[:, :])
                        ins.then_inc(s_xln_ps, 1)
                    if isinstance(c, int) and c == -1 and p in (1, 2):
                        pe.wait_ge(s_wready, 6)
                        transpose_layers(p - 1)
                    if p == 1 and live(c + 2):
                        pe.wait_ge(s_q_hi, c + 3)
                        nc.tensor.matmul(work0[:, :], neg_ident[:, :], parts[par][:, 0, 0, :], start=False, stop=True,
                                         skip_group_check=True).then_inc(s_q_rest, 1)
                    if p == 2 and live(c + 2):
                        pe.wait_ge(s_k_hi, c + 3)
                        nc.tensor.matmul(work1[:, :], neg_ident[:, :], parts[par][:, 1, 0, :], start=False, stop=True,
                                         skip_group_check=True).then_inc(s_k_rest, 1)
                    early_steps(c, p, step)

            def transpose_z(v, k, dst, i=0):
                pe.wait_ge(p_z[v], k + 1)
                for t in range(TPC):
                    ins = nc.tensor.transpose(dst[:, TILE * t:TILE * (t + 1)], z[v][i][:, t, :], ident[:, :])
                ins.then_inc(p_zt[v], 1)

            def first_layer(v, hk, dst):
                bias_rows(dst, 1 + v)
                for t in range(TPC):
                    ins = nc.tensor.matmul(dst[:, TILE * t:TILE * (t + 1)], hk[:, TILE * t:TILE * (t + 1)],
                                           lin_t[:, 2 * v - 2, :], start=False, stop=True, skip_group_check=True)
                ins.then_inc(p_y[v], 1)

            def step(t, par):
                if isinstance(t, int):
                    if t == 1:
                        pe.wait_ge(s_k_lo, NCHUNK)
                    elif t == 2:
                        pe.wait_ge(s_v, NCHUNK)
                    elif t == 3:
                        pe.wait_ge(s_exp, PPC * NCHUNK)
                    elif t == FIRST_STEP:
                        pe.wait_ge(s_x2, NCHUNK)
                for v, k in ((3, t - 6), (2, t - 4), (1, t - 2)):
                    if v == 2 and live(t - 7):
                        if live(t - 6):
                            pe.wait_ge(p_h[2], t - 5)
                        transpose_z(3, t - 7, transpose_bank(3, t, par))
                    if live(k):
                        pe.wait_ge(p_h[v - 1], k + 1)
                        if v > 1 or (isinstance(t, int) and t <= FIRST_STEP):
                            if some(k):
                                pe.wait_ge(p_z[v], k)
                        elif live(t - 8):
                            pe.wait_ge(p_out, t - 7)
                        first_layer(v, h[v - 1][(par - 2 * v) % 2], first_layer_bank(v, t, par))
                if live(t - 5):
                    if live(t - 4):
                        pe.wait_ge(p_h[1], t - 3)
                    transpose_z(2, t - 5, transpose_bank(2, t, par))
                if live(t - 3):
                    transpose_z(1, t - 3, transpose_bank(1, t, par))
                if live(t - 1):
                    if some(t - 1):
                        pe.wait_ge(p_h[0], t - 1)
                    transpose_z(0, t - 1, bank[7], 1 - par)
                for v, k in ((3, t - 7), (2, t - 5), (1, t - 3)):
                    if live(k):
                        pe.wait_ge(p_g[v], k + 1)
                        if some(k):
                            pe.wait_ge(p_h[v], k)
                        nc.tensor.matmul(second_layer_bank(v, t), lin_t[:, 2 * v - 1, :], g[v - 1][:, :], start=True,
                                         stop=True).then_inc(p_c[v], 1)
                if live(t - 7):
                    pe.wait_ge(p_h[3], t - 6)
                    for i in range(TPC):
                        ins = nc.tensor.transpose(last_bank(par)[:, TILE * i:TILE * (i + 1)],
                                                  h[3][0][:, TILE * i:TILE * (i + 1)], ident[:, :])
                    ins.then_inc(p_ht, 1)

            chunks(pe, chunk)
            steps(pe, step)


_INS = ["x", "ctx_1024", "L0_xattn_Wk_w", "L0_xattn_Wk_b", "L0_xattn_Wq_w", "L0_xattn_Wq_b", "L0_xattn_Wv_w",
        "L0_xattn_Wv_b", "L0_xattn_Wo_w", "L0_xattn_Wo_b", "L0_ffn_qweights", "L0_ffn_scales", "L0_ffn_biases",
        "L0_ffn_lora_a", "L0_ffn_lora_b", "L0_ffn_ln_gamma", "L0_ffn_ln_beta"]


def kernel(**inputs):
    import numpy as _np
    import concourse.bacc as _bacc
    from concourse import mybir as _mybir
    from concourse.bass_utils import run_bass_kernel_spmd as _run

    nc = _bacc.Bacc("TRN2", target_bir_lowering=False, num_devices=1)
    arrays, args = {}, []
    for name in _INS:
        a = _np.ascontiguousarray(inputs[name])
        arrays[f"in_{name}"] = a
        args.append(nc.dram_tensor(f"in_{name}", a.shape, _mybir.dt.from_np(a.dtype), kind="ExternalInput").ap())
    args.append(nc.dram_tensor("out_0", (BATCH, SEQ, D), F32, kind="ExternalOutput").ap())
    build(nc, *args)
    r = _run(nc, [arrays], core_ids=[0])
    return r.results[0]["out_0"]
```
